# Optimizing a Trainium2 kernel written in Bass

```python
import numpy as np
import jax
import jax.numpy as jnp

def _softmax(x, axis=-1):
    return jax.nn.softmax(x, axis=axis)

def _gelu(x):
    return jax.nn.gelu(x, approximate=True)

def _silu(x):
    return jax.nn.silu(x)

def _sigmoid(x):
    return jax.nn.sigmoid(x)

def _layernorm(x, axis=-1, eps=1e-05):
    m = jnp.mean(x, axis=axis, keepdims=True)
    v = jnp.var(x, axis=axis, keepdims=True)
    return (x - m) / jnp.sqrt(v + eps)

def _scatter_add(tgt, idx, src, axis=0):
    return tgt.at[idx].add(src)

def _segment_sum(src, seg, n):
    return jax.ops.segment_sum(src, seg, n)
kernel_name = 'mk_perceiver_d2_seqx_r8_8d0760'

def setup_inputs(seed: int=0):
    np.random.seed(seed)
    _w = jnp.asarray

    def _rec_inputs():
        import jax
        import jax.numpy as jnp
        _rk = jax.random.key(seed)
        x = 7.22e-05 + 1 * jax.random.normal(jax.random.fold_in(_rk, 1), (32, 64, 256), jnp.float32)
        _lenS = 64 - jax.random.randint(jax.random.fold_in(_rk, 7), (32,), 0, max(1, 64 // 4) + 1, jnp.int32)
        _lenS2 = 1601 - jax.random.randint(jax.random.fold_in(_rk, 8), (32,), 0, max(1, 1601 // 4) + 1, jnp.int32)
        _ctx_512P = jax.random.normal(jax.random.fold_in(_rk, 11), (32, 16, 64), jnp.float32)
        _ctx_512c = jax.random.dirichlet(jax.random.fold_in(_rk, 511), 0.3 * jnp.ones((16,), jnp.float32), (32, 1601))
        _ctx_512t = jnp.einsum('bsk,bkd->bsd', _ctx_512c, _ctx_512P)
        _ctx_512t = _ctx_512t * jax.lax.rsqrt(jnp.mean(jnp.square(_ctx_512t)) + 1e-12) * 0.953939
        ctx_512 = -0.000514642 + 1.00011 * (_ctx_512t + 0.3 * jax.random.normal(jax.random.fold_in(_rk, 611), (32, 1601, 64), jnp.float32))
        return (x, ctx_512)
    x, ctx_512 = _rec_inputs()

    def _L0_xattn_setup():
        import jax, jax.numpy as jnp
        import numpy as np
        B, S, H, NH, L = (2, 256, 256, 16, 64)
        HD = H // NH
        key = jax.random.key(seed)
        k1, k2, k3, k4, k5 = jax.random.split(key, 5)
        scale = 0.02
        return {'q': jax.random.normal(k1, (B, S, H), dtype=jnp.float32), 'latent_kv': jax.random.normal(k2, (B, S, L), dtype=jnp.float32), 'Wq': jax.random.normal(k3, (H, H), dtype=jnp.float32) * scale, 'Wkv_expand': jax.random.normal(k4, (2 * H, L), dtype=jnp.float32) * scale, 'Wout': jax.random.normal(k5, (H, H), dtype=jnp.float32) * scale}
    _L0_xattn_all = _L0_xattn_setup()
    _L0_xattn_in = {k: v for k, v in _L0_xattn_all.items() if k in ('Wq', 'Wkv_expand', 'Wout')}
    del _L0_xattn_all

    def _L0_attn_setup():
        import jax, jax.numpy as jnp
        import numpy as np
        N_HEADS = 16
        key = jax.random.key(seed)
        ks = jax.random.split(key, 9)
        B, S, D = (2, 256, 256)
        s = 0.02
        return {'X': jax.random.normal(ks[0], (B, S, D), jnp.float32), 'Wq': jax.random.normal(ks[1], (D, D), jnp.float32) * s, 'bq': jax.random.normal(ks[2], (D,), jnp.float32) * s, 'Wk': jax.random.normal(ks[3], (D, D), jnp.float32) * s, 'bk': jax.random.normal(ks[4], (D,), jnp.float32) * s, 'Wv': jax.random.normal(ks[5], (D, D), jnp.float32) * s, 'bv': jax.random.normal(ks[6], (D,), jnp.float32) * s, 'Wo': jax.random.normal(ks[7], (D, D), jnp.float32) * s, 'bo': jax.random.normal(ks[8], (D,), jnp.float32) * s}
    _L0_attn_all = _L0_attn_setup()
    _L0_attn_in = {k: v for k, v in _L0_attn_all.items() if k in ('Wq', 'bq', 'Wk', 'bk', 'Wv', 'bv', 'Wo', 'bo')}
    del _L0_attn_all

    def _L0_ffn_setup():
        import jax, jax.numpy as jnp
        import numpy as np
        import math
        GELU_C = math.sqrt(2.0 / math.pi)

        def activation_quant(x):
            scale = 127.0 / jnp.clip(jnp.max(jnp.abs(x), axis=-1, keepdims=True), 1e-05, None)
            y = jnp.clip(jnp.round(x * scale), -128, 127) / scale
            return x + jax.lax.stop_gradient(y - x)

        def weight_quant(w):
            scale = jnp.clip(jnp.mean(jnp.abs(w), axis=-1, keepdims=True), 1e-05, None)
            quant = jnp.clip(jnp.round(w / scale), -1, 1) * scale
            w_q = w + jax.lax.stop_gradient(quant - w)
            return (w_q / scale, scale.T)

        def new_gelu(x):
            return 0.5 * x * (1.0 + jnp.tanh(GELU_C * (x + 0.044715 * x * x * x)))

        def bitlinear(x, w):
            x_q = activation_quant(x)
            w_q, scale = weight_quant(w)
            out = jnp.einsum('bsd,hd->bsh', x_q, w_q)
            return out * scale
        key = jax.random.key(seed)
        k1, k2, k3 = jax.random.split(key, 3)
        dim, hidden = (256, 1024)
        B, S = (4, 256)
        x = jax.random.normal(k1, (B, S, dim), dtype=jnp.float32)
        lim1 = 1.0 / math.sqrt(dim)
        lim2 = 1.0 / math.sqrt(hidden)
        w1 = jax.random.uniform(k2, (hidden, dim), dtype=jnp.float32, minval=-lim1, maxval=lim1)
        w2 = jax.random.uniform(k3, (dim, hidden), dtype=jnp.float32, minval=-lim2, maxval=lim2)
        return {'x': x, 'w1': w1, 'w2': w2}
    _L0_ffn_all = _L0_ffn_setup()
    _L0_ffn_in = {k: v for k, v in _L0_ffn_all.items() if k in ('w1', 'w2')}
    del _L0_ffn_all

    def _L1_xattn_setup():
        import jax, jax.numpy as jnp
        import numpy as np
        B, S, L = (2, 128, 128)
        DIM_Q, H, K, D_C, D_CQ, R = (256, 16, 128, 64, 192, 64)

        def _rope_tables(length, dim):
            inv = 1.0 / 10000.0 ** (jnp.arange(0, dim, 2, dtype=jnp.float32) / dim)
            f = jnp.arange(length, dtype=jnp.float32)[:, None] * inv[None, :]
            sin = jnp.repeat(jnp.sin(f), 2, axis=-1)
            cos = jnp.repeat(jnp.cos(f), 2, axis=-1)
            return (sin, cos)

        def _rotate_half(x):
            half = x.shape[-1] // 2
            return jnp.concatenate([-x[..., half:], x[..., :half]], axis=-1)

        def _apply_rope(x, sin, cos):
            return x * cos + _rotate_half(x) * sin
        key = jax.random.key(seed)
        ks = jax.random.split(key, 8)
        return {'hidden_q': jax.random.normal(ks[0], (B, S, DIM_Q), jnp.float32), 'kv_c': jax.random.normal(ks[1], (B, L, D_C), jnp.float32), 'Wq': jax.random.normal(ks[2], (H * K, DIM_Q), jnp.float32) / np.sqrt(DIM_Q).astype(np.float32), 'w_kc_q': jax.random.normal(ks[3], (H, K, D_CQ), jnp.float32) / np.sqrt(K).astype(np.float32), 'w_kc_kv': jax.random.normal(ks[4], (H, K, D_C), jnp.float32) / np.sqrt(K).astype(np.float32), 'W_qr': jax.random.normal(ks[5], (H, D_CQ, R), jnp.float32) / np.float32(np.sqrt(D_CQ) * np.sqrt(R)), 'W_kr': jax.random.normal(ks[6], (H, D_C, R), jnp.float32) / np.sqrt(D_C).astype(np.float32), 'Wo': jax.random.normal(ks[7], (DIM_Q, H * K), jnp.float32) / np.sqrt(H * K).astype(np.float32)}
    _L1_xattn_all = _L1_xattn_setup()
    _L1_xattn_in = {k: v for k, v in _L1_xattn_all.items() if k in ('Wq', 'w_kc_q', 'w_kc_kv', 'W_qr', 'W_kr', 'Wo')}
    del _L1_xattn_all

    def _L1_attn_setup():
        import jax, jax.numpy as jnp
        import numpy as np
        B, T, D, H = (2, 256, 256, 16)
        DH = D // H
        ROPE_BASE = 10000.0

        def _rope(x, cos, sin):
            x0 = x[..., 0::2]
            x1 = x[..., 1::2]
            r0 = cos * x0 - sin * x1
            r1 = sin * x0 + cos * x1
            return jnp.stack((r0, r1), axis=-1).reshape(x.shape)
        key = jax.random.key(seed)
        ks = jax.random.split(key, 5)
        s = D ** (-0.5)
        return {'X': jax.random.normal(ks[0], (B, T, D), dtype=jnp.float32), 'Wq': jax.random.normal(ks[1], (D, D), dtype=jnp.float32) * s, 'Wk': jax.random.normal(ks[2], (D, D), dtype=jnp.float32) * s, 'Wv': jax.random.normal(ks[3], (D, D), dtype=jnp.float32) * s, 'Wo': jax.random.normal(ks[4], (D, D), dtype=jnp.float32) * s}
    _L1_attn_all = _L1_attn_setup()
    _L1_attn_in = {k: v for k, v in _L1_attn_all.items() if k in ('Wq', 'Wk', 'Wv', 'Wo')}
    del _L1_attn_all

    def _L1_ffn_setup():
        import jax, jax.numpy as jnp
        import numpy as np
        TOP_K = 4

        def _silu_and_mul(gu):
            g, u = jnp.split(gu, 2, axis=-1)
            return jax.nn.silu(g) * u
        key = jax.random.key(seed)
        ks = jax.random.split(key, 7)
        H, E, I, Is = (256, 16, 176, 704)
        s = 0.02
        return {'hidden_states': jax.random.normal(ks[0], (4, 128, H), dtype=jnp.float32), 'gate_w': jax.random.normal(ks[1], (E, H), dtype=jnp.float32) * s, 'sgate_w': jax.random.normal(ks[2], (1, H), dtype=jnp.float32) * s, 'w13': jax.random.normal(ks[3], (E, 2 * I, H), dtype=jnp.float32) * s, 'w2': jax.random.normal(ks[4], (E, H, I), dtype=jnp.float32) * s, 'shared_gate_up_w': jax.random.normal(ks[5], (2 * Is, H), dtype=jnp.float32) * s, 'shared_down_w': jax.random.normal(ks[6], (H, Is), dtype=jnp.float32) * s}
    _L1_ffn_all = _L1_ffn_setup()
    _L1_ffn_in = {k: v for k, v in _L1_ffn_all.items() if k in ('gate_w', 'sgate_w', 'w13', 'w2', 'shared_gate_up_w', 'shared_down_w')}
    del _L1_ffn_all
    return {'x': x, 'ctx_512': ctx_512, 'L0_xattn_Wq': _L0_xattn_in['Wq'], 'L0_xattn_Wkv_expand': _L0_xattn_in['Wkv_expand'], 'L0_xattn_Wout': _L0_xattn_in['Wout'], 'L0_attn_Wq': _L0_attn_in['Wq'], 'L0_attn_bq': _L0_attn_in['bq'], 'L0_attn_Wk': _L0_attn_in['Wk'], 'L0_attn_bk': _L0_attn_in['bk'], 'L0_attn_Wv': _L0_attn_in['Wv'], 'L0_attn_bv': _L0_attn_in['bv'], 'L0_attn_Wo': _L0_attn_in['Wo'], 'L0_attn_bo': _L0_attn_in['bo'], 'L0_ffn_w1': _L0_ffn_in['w1'], 'L0_ffn_w2': _L0_ffn_in['w2'], 'L1_xattn_Wq': _L1_xattn_in['Wq'], 'L1_xattn_w_kc_q': _L1_xattn_in['w_kc_q'], 'L1_xattn_w_kc_kv': _L1_xattn_in['w_kc_kv'], 'L1_xattn_W_qr': _L1_xattn_in['W_qr'], 'L1_xattn_W_kr': _L1_xattn_in['W_kr'], 'L1_xattn_Wo': _L1_xattn_in['Wo'], 'L1_attn_Wq': _L1_attn_in['Wq'], 'L1_attn_Wk': _L1_attn_in['Wk'], 'L1_attn_Wv': _L1_attn_in['Wv'], 'L1_attn_Wo': _L1_attn_in['Wo'], 'L1_ffn_gate_w': _L1_ffn_in['gate_w'], 'L1_ffn_sgate_w': _L1_ffn_in['sgate_w'], 'L1_ffn_w13': _L1_ffn_in['w13'], 'L1_ffn_w2': _L1_ffn_in['w2'], 'L1_ffn_shared_gate_up_w': _L1_ffn_in['shared_gate_up_w'], 'L1_ffn_shared_down_w': _L1_ffn_in['shared_down_w']}

def reference(x, ctx_512, L0_xattn_Wq, L0_xattn_Wkv_expand, L0_xattn_Wout, L0_attn_Wq, L0_attn_bq, L0_attn_Wk, L0_attn_bk, L0_attn_Wv, L0_attn_bv, L0_attn_Wo, L0_attn_bo, L0_ffn_w1, L0_ffn_w2, L1_xattn_Wq, L1_xattn_w_kc_q, L1_xattn_w_kc_kv, L1_xattn_W_qr, L1_xattn_W_kr, L1_xattn_Wo, L1_attn_Wq, L1_attn_Wk, L1_attn_Wv, L1_attn_Wo, L1_ffn_gate_w, L1_ffn_sgate_w, L1_ffn_w13, L1_ffn_w2, L1_ffn_shared_gate_up_w, L1_ffn_shared_down_w):
    import jax
    import jax.numpy as jnp

    def _L0_xattn_ref(q, latent_kv, Wq, Wkv_expand, Wout):
        import jax, jax.numpy as jnp
        import numpy as np
        B, S, H, NH, L = (2, 256, 256, 16, 64)
        HD = H // NH
        b, sq, _ = q.shape
        sk = latent_kv.shape[1]
        qp = q @ Wq.T
        kv = latent_kv @ Wkv_expand.T
        k, v = jnp.split(kv, 2, axis=-1)
        qh = qp.reshape(b, sq, NH, HD).transpose(0, 2, 1, 3)
        kh = k.reshape(b, sk, NH, HD).transpose(0, 2, 1, 3)
        vh = v.reshape(b, sk, NH, HD).transpose(0, 2, 1, 3)
        inv_sqrt_d = 1.0 / jnp.sqrt(jnp.float32(HD))
        scores = jnp.einsum('bhqd,bhkd->bhqk', qh, kh) * inv_sqrt_d
        causal = jnp.tril(jnp.ones((sq, sk), dtype=bool))
        scores = jnp.where(causal, scores, jnp.finfo(scores.dtype).min)
        attn = jax.nn.softmax(scores, axis=-1)
        out = jnp.einsum('bhqk,bhkd->bhqd', attn, vh)
        out = out.transpose(0, 2, 1, 3).reshape(b, sq, H)
        return out @ Wout.T

    def _L0_attn_ref(X, Wq, bq, Wk, bk, Wv, bv, Wo, bo):
        import jax, jax.numpy as jnp
        import numpy as np
        N_HEADS = 16
        B, S, D = X.shape
        H = N_HEADS
        d_head = D // H
        scale = jnp.asarray(1.0 / np.sqrt(np.sqrt(d_head)), X.dtype)
        Q = (X @ Wq.T + bq).reshape(B, S, H, d_head) * scale
        K = (X @ Wk.T + bk).reshape(B, S, H, d_head) * scale
        V = (X @ Wv.T + bv).reshape(B, S, H, d_head)
        scores = jnp.einsum('bqhd,bkhd->bhqk', Q, K)
        causal = jnp.tril(jnp.ones((S, S), bool))
        scores = jnp.where(causal[None, None], scores, -jnp.inf)
        attn = jax.nn.softmax(scores.astype(jnp.float32), axis=-1).astype(X.dtype)
        out = jnp.einsum('bhqk,bkhd->bqhd', attn, V).reshape(B, S, D)
        return out @ Wo.T + bo

    def _L0_ffn_ref(x, w1, w2):
        import jax, jax.numpy as jnp
        import numpy as np
        import math
        GELU_C = math.sqrt(2.0 / math.pi)

        def activation_quant(x):
            scale = 127.0 / jnp.clip(jnp.max(jnp.abs(x), axis=-1, keepdims=True), 1e-05, None)
            y = jnp.clip(jnp.round(x * scale), -128, 127) / scale
            return x + jax.lax.stop_gradient(y - x)

        def weight_quant(w):
            scale = jnp.clip(jnp.mean(jnp.abs(w), axis=-1, keepdims=True), 1e-05, None)
            quant = jnp.clip(jnp.round(w / scale), -1, 1) * scale
            w_q = w + jax.lax.stop_gradient(quant - w)
            return (w_q / scale, scale.T)

        def new_gelu(x):
            return 0.5 * x * (1.0 + jnp.tanh(GELU_C * (x + 0.044715 * x * x * x)))

        def bitlinear(x, w):
            x_q = activation_quant(x)
            w_q, scale = weight_quant(w)
            out = jnp.einsum('bsd,hd->bsh', x_q, w_q)
            return out * scale
        h = bitlinear(x, w1)
        h = new_gelu(h)
        return bitlinear(h, w2)

    def _L1_xattn_ref(hidden_q, kv_c, Wq, w_kc_q, w_kc_kv, W_qr, W_kr, Wo):
        import jax, jax.numpy as jnp
        import numpy as np
        B, S, L = (2, 128, 128)
        DIM_Q, H, K, D_C, D_CQ, R = (256, 16, 128, 64, 192, 64)

        def _rope_tables(length, dim):
            inv = 1.0 / 10000.0 ** (jnp.arange(0, dim, 2, dtype=jnp.float32) / dim)
            f = jnp.arange(length, dtype=jnp.float32)[:, None] * inv[None, :]
            sin = jnp.repeat(jnp.sin(f), 2, axis=-1)
            cos = jnp.repeat(jnp.cos(f), 2, axis=-1)
            return (sin, cos)

        def _rotate_half(x):
            half = x.shape[-1] // 2
            return jnp.concatenate([-x[..., half:], x[..., :half]], axis=-1)

        def _apply_rope(x, sin, cos):
            return x * cos + _rotate_half(x) * sin
        Bv, Sv, _ = hidden_q.shape
        _, Lv, _ = kv_c.shape
        q_hk = (hidden_q @ Wq.T).reshape(Bv, Sv, H, K)
        q_big = jnp.einsum('bshk,hkq->bshq', q_hk, w_kc_q)
        sin_q, cos_q = _rope_tables(Sv, D_CQ)
        q_big = _apply_rope(q_big, sin_q[None, :, None, :], cos_q[None, :, None, :])
        sin_k, cos_k = _rope_tables(Lv, D_C)
        kv_r = _apply_rope(kv_c, sin_k[None], cos_k[None])
        q_r = jnp.einsum('bshq,hqr->bhsr', q_big, W_qr)
        k_r = jnp.einsum('bld,hdr->bhlr', kv_r, W_kr)
        scores = jnp.einsum('bhsr,bhlr->bhsl', q_r, k_r)
        attn = jax.nn.softmax(scores, axis=-1)
        ctx_c = jnp.einsum('bhsl,bld->bhsd', attn, kv_r)
        ctx_lat = jnp.einsum('bhsd,hkd->bhsk', ctx_c, w_kc_kv)
        ctx = ctx_lat.transpose(0, 2, 1, 3).reshape(Bv, Sv, H * K)
        return ctx @ Wo.T

    def _L1_attn_ref(X, Wq, Wk, Wv, Wo):
        import jax, jax.numpy as jnp
        import numpy as np
        B, T, D, H = (2, 256, 256, 16)
        DH = D // H
        ROPE_BASE = 10000.0

        def _rope(x, cos, sin):
            x0 = x[..., 0::2]
            x1 = x[..., 1::2]
            r0 = cos * x0 - sin * x1
            r1 = sin * x0 + cos * x1
            return jnp.stack((r0, r1), axis=-1).reshape(x.shape)
        b, t, d = X.shape
        Q = X @ Wq.T
        K = X @ Wk.T
        V = X @ Wv.T
        Qh = Q.reshape(b, t, H, DH).transpose(0, 2, 1, 3)
        Kh = K.reshape(b, t, H, DH).transpose(0, 2, 1, 3)
        Vh = V.reshape(b, t, H, DH).transpose(0, 2, 1, 3)
        theta = ROPE_BASE ** (-2.0 * jnp.arange(DH // 2, dtype=jnp.float32) / DH)
        angles = jnp.arange(t, dtype=jnp.float32)[:, None] * theta[None, :]
        cos = jnp.cos(angles).astype(X.dtype)
        sin = jnp.sin(angles).astype(X.dtype)
        Qr = _rope(Qh, cos, sin)
        Kr = _rope(Kh, cos, sin)
        scores = jnp.einsum('bhqd,bhkd->bhqk', Qr, Kr) * DH ** (-0.5)
        causal = jnp.triu(jnp.ones((t, t), dtype=bool), 1)
        scores = jnp.where(causal, jnp.finfo(scores.dtype).min, scores)
        pattern = jax.nn.softmax(scores, axis=-1)
        heads = jnp.einsum('bhqk,bhkd->bqhd', pattern, Vh).reshape(b, t, d)
        return heads @ Wo.T

    def _L1_ffn_ref(hidden_states, gate_w, sgate_w, w13, w2, shared_gate_up_w, shared_down_w):
        import jax, jax.numpy as jnp
        import numpy as np
        TOP_K = 4

        def _silu_and_mul(gu):
            g, u = jnp.split(gu, 2, axis=-1)
            return jax.nn.silu(g) * u
        B, S, H = hidden_states.shape
        x = hidden_states.reshape(-1, H)
        E = gate_w.shape[0]
        shared = _silu_and_mul(x @ shared_gate_up_w.T) @ shared_down_w.T
        shared = shared * jax.nn.sigmoid(x @ sgate_w.T)
        router_logits = x @ gate_w.T
        routing_weights = jax.nn.softmax(router_logits.astype(jnp.float32), axis=-1)
        topk_w, topk_ids = jax.lax.top_k(routing_weights, TOP_K)

        def body(acc, ew):
            w13_e, w2_e, e = ew
            coef = jnp.sum(jnp.where(topk_ids == e, topk_w, 0.0), axis=-1)
            h = _silu_and_mul(x @ w13_e.T)
            acc = acc + (h @ w2_e.T).astype(jnp.float32) * coef[:, None]
            return (acc, None)
        init = jnp.zeros((x.shape[0], H), dtype=jnp.float32)
        sparse_out, _ = jax.lax.scan(body, init, (w13, w2, jnp.arange(E)))
        out = shared + sparse_out.astype(x.dtype)
        return out.reshape(B, S, H)
    x = x + _L0_xattn_ref(_layernorm(x, axis=-1), ctx_512, L0_xattn_Wq, L0_xattn_Wkv_expand, L0_xattn_Wout)
    x = x + _L0_attn_ref(_layernorm(x, axis=-1), L0_attn_Wq, L0_attn_bq, L0_attn_Wk, L0_attn_bk, L0_attn_Wv, L0_attn_bv, L0_attn_Wo, L0_attn_bo)
    x = x + _L0_ffn_ref(_layernorm(x, axis=-1), L0_ffn_w1, L0_ffn_w2)
    x = x + _L1_xattn_ref(_layernorm(x, axis=-1), ctx_512, L1_xattn_Wq, L1_xattn_w_kc_q, L1_xattn_w_kc_kv, L1_xattn_W_qr, L1_xattn_W_kr, L1_xattn_Wo)
    x = x + _L1_attn_ref(_layernorm(x, axis=-1), L1_attn_Wq, L1_attn_Wk, L1_attn_Wv, L1_attn_Wo)
    x = x + _L1_ffn_ref(_layernorm(x, axis=-1), L1_ffn_gate_w, L1_ffn_sgate_w, L1_ffn_w13, L1_ffn_w2, L1_ffn_shared_gate_up_w, L1_ffn_shared_down_w)
    return x

_drawn_inputs = setup_inputs


def setup_inputs(seed=0):
    import zlib

    import numpy as np

    out = dict(_drawn_inputs(seed))
    spreads = {}
    factors = {'L0_xattn_Wq': 26.228,
     'L0_attn_Wq': 8.0,
     'L0_attn_bq': 8.0,
     'L0_attn_Wk': 8.0,
     'L0_attn_bk': 64.0,
     'L0_attn_bv': 6.703,
     'L1_ffn_gate_w': 8.0,
     'L1_ffn_sgate_w': 8.0,
     'L1_ffn_w13': 8.0,
     'L1_ffn_w2': 8.0,
     'L1_ffn_shared_gate_up_w': 4.434,
     'L1_ffn_shared_down_w': 4.438}
    for name, (base, spread) in spreads.items():
        noise = np.random.default_rng([zlib.crc32(name.encode()), seed]).standard_normal(out[name].shape)
        drawn = base * np.exp(spread * noise) if base else spread * noise
        out[name] = jnp.asarray(drawn.astype(out[name].dtype))
    for name, factor in factors.items():
        out[name] = (out[name] * factor).astype(out[name].dtype)
    return out
```

```python
import math
from contextlib import ExitStack

import numpy as np

import concourse.bass as bass
from concourse import mybir

F32 = mybir.dt.float32
F32R = mybir.dt.float32r
BF16 = mybir.dt.bfloat16
ALU = mybir.AluOpType
ACT = mybir.ActivationFunctionType
AX = mybir.AxisListType

P = 128
B, S, D = 32, 64, 256
NT = B * S // P
DC = D // P
H, DH = 16, 16
NP = H // 2
SLOTS = 2
ROUNDS = NT // SLOTS
EPS = 1e-5
SK = 1601
DCX = 64
FF = 1024
ROUND = 1.5 * 2.0 ** 23
VW = 2 * DH + 2


LEAD = 1


class Steps:

    def __init__(self, engine, sem):
        self.engine, self.sem, self.base, self.n = engine, sem, 0, 0

    def start(self, base):
        self.base, self.n = base, 0

    def done(self, instruction):
        instruction.then_inc(self.sem, 1)
        self.n += 1
        self.engine.wait_ge(self.sem, self.base + self.n)


def small_attention(nc, sb, pb, sem, kind, name, w, x_all, const, nth, steps_before):
    ident, mask, head_rows = const["ident"], const["mask"], const["head_rows"]
    G = range(SLOTS)
    before = nth * NT

    stats = [sb(f"{name}_stats{g}", [P, 6]) for g in G]
    mv = [sb(f"{name}_mv{g}", [P, 3]) for g in G]
    rstd = [sb(f"{name}_rstd{g}", [P, 1]) for g in G]
    xn = [sb(f"{name}_xn{g}", [P, D]) for g in G]
    xnT = [sb(f"{name}_xnT{g}", [P, DC, P]) for g in G]
    qk = [sb(f"{name}_qk{g}", [P, 2 * D]) for g in G]
    kT = [sb(f"{name}_kT{g}", [P, DC, P]) for g in G]
    qbd = [sb(f"{name}_qbd{g}", [P, DC, H // 2, P]) for g in G]
    vbd = [sb(f"{name}_vbd{g}", [P, 2, NP, VW]) for g in G]
    prob = [sb(f"{name}_prob{g}", [P, H, S]) for g in G]
    rmax = [sb(f"{name}_rmax{g}", [P, H]) for g in G]
    probT = [sb(f"{name}_probT{g}", [P, NP, P]) for g in G]
    rden = [sb(f"{name}_rden{g}", [P, H]) for g in G]
    heads = [sb(f"{name}_heads{g}", [P, D]) for g in G]
    headsT = [sb(f"{name}_headsT{g}", [P, DC, P]) for g in G]
    front = [pb(f"{name}_front{g}", [P, 512]) for g in G]
    vps = [pb(f"{name}_v{g}", [P, 2, D]) for g in G]
    score = [pb(f"{name}_score{g}", [P, 2, 512]) for g in G]
    if kind == "context":
        ctxT = [sb(f"{name}_ctxT{g}", [DCX, P]) for g in G]
    if kind == "rope":
        t1 = [sb(f"{name}_t1{g}", [P, 2 * D]) for g in G]
        t2 = [sb(f"{name}_t2{g}", [P, 2 * D]) for g in G]

    s_var = sem("attention_variance")
    s_rstd = sem("attention_rstd")
    s_xn = sem("attention_normalised")
    s_xT = sem("attention_x_turned")
    s_xTc = sem("attention_xT_kept")
    s_ctx = sem("attention_ctx_tile")
    s_qk = sem("attention_qk_made")
    s_v = sem("attention_v_made")
    s_qkc = sem("attention_qk_kept")
    s_vc = sem("attention_v_kept")
    s_qT = sem("attention_q_turned")
    s_kT = sem("attention_k_turned")
    s_kTc = sem("attention_kT_kept")
    s_qbd = sem("attention_q_spread")
    s_sc = sem("attention_scores")
    s_shift = sem("attention_shifted")
    s_exp = sem("attention_exp")
    s_pT = sem("attention_probs_turned")
    s_pTa = sem("attention_probT_kept_act")
    s_pTd = sem("attention_probT_kept_dve")
    s_o = sem("attention_heads_made")
    s_on = sem("attention_heads_scaled")
    s_oT = sem("attention_heads_turned")
    s_oTc = sem("attention_headsT_kept")
    s_y = sem("attention_out_made")
    s_x = sem("attention_x_updated")
    s_one = sem("attention_ones_set")
    s_dve = sem("attention_dve_step")
    dve_steps = SLOTS * {"context": 5, "bias": 6, "rope": 6}[kind]

    with nc.Block() as block:

        @block.gpsimd
        def _(pool):
            for g in G:
                pool.memset(vbd[g][:, :, :, :], 0.0).then_inc(s_one, 1)
            pool.wait_ge(s_one, 3 * SLOTS * nth + SLOTS)
            for g in G:
                pool.memset(vbd[g][0:S, :, :, 2 * DH:2 * DH + 1], 1.0).then_inc(s_one, 1)
                pool.memset(vbd[g][S:P, :, :, 2 * DH + 1:VW], 1.0).then_inc(s_one, 1)
            pool.wait_ge(s_one, 3 * SLOTS * (nth + 1))
            with pool.Fori(0, ROUNDS) as r:
                for g in G:
                    if kind == "context":
                        pool.wait_ge(s_qk, LEAD + r * SLOTS)
                        pool.wait_ge(s_v, LEAD + r * SLOTS)
                        pool.tensor_copy(ctxT[g][:, :], w["ctx"][:, bass.ds((r * SLOTS + g) * P, P)])\
                            .then_inc(s_ctx, 1)
                for g in G:
                    pool.wait_ge(s_var, r * SLOTS + before + g + 1)
                    pool.tensor_tensor(rstd[g][:, :], mv[g][:, 1:2], const["minus_half"][:, 0:1], ALU.pow)\
                        .then_inc(s_rstd, 1)

        @block.tensor
        def _(pe):
            if nth == 0:
                pe.sem_inc(s_qk, LEAD)
                pe.sem_inc(s_v, LEAD)

            def turn_x(r, g):
                pe.wait_ge(s_xn, r * SLOTS + before + g + 1)
                for c in range(DC):
                    last = pe.transpose(front[g][:, c * P:(c + 1) * P], xn[g][:, c * P:(c + 1) * P], ident[:, :])
                last.then_inc(s_xT, 1)

            def project(r, g):
                pe.wait_ge(s_xTc, r * SLOTS + before + g + 1)
                if kind == "context":
                    pe.wait_ge(s_ctx, r * SLOTS + before + g + 1)
                    for c in range(DC):
                        pe.matmul(front[g][:, 0:D], xnT[g][:, c, :], w["q"][:, c, :],
                                  start=(c == 0), stop=(c == DC - 1))
                    last = pe.matmul(front[g][:, D:2 * D], ctxT[g][:, :], w["k"][:, :], start=True, stop=True)
                else:
                    for c in range(DC):
                        last = pe.matmul(front[g][:, :], xnT[g][:, c, :], w["qk"][:, c, :],
                                         start=(c == 0), stop=(c == DC - 1))
                last.then_inc(s_qk, 1)
                for b in range(2):
                    for half in range(2):
                        o = vps[g][S * half:S * half + S, b, :]
                        if kind == "context":
                            last = pe.matmul(o, ctxT[g][:, b * S:(b + 1) * S], w["v"][:, :], start=True, stop=True)
                        else:
                            for c in range(DC):
                                last = pe.matmul(o, xnT[g][:, c, b * S:(b + 1) * S], w["v"][:, c, :],
                                                 start=(c == 0), stop=(c == DC - 1))
                last.then_inc(s_v, 1)

            def turn_qk(r, g):
                pe.wait_ge(s_qkc, r * SLOTS + before + g + 1)
                for c in range(DC):
                    last = pe.transpose(front[g][:, c * P:(c + 1) * P], qk[g][:, c * P:(c + 1) * P], ident[:, :])
                last.then_inc(s_qT, 1)
                pe.wait_ge(s_vc, r * SLOTS + before + g + 1)
                for c in range(DC):
                    last = pe.transpose(vps[g][:, 0, c * P:(c + 1) * P],
                                        qk[g][:, D + c * P:D + (c + 1) * P], ident[:, :])
                last.then_inc(s_kT, 1)

            def scores(r, g):
                pe.wait_ge(s_kTc, r * SLOTS + before + g + 1)
                pe.wait_ge(s_qbd, r * SLOTS + before + g + 1)
                pe.wait_ge(s_x, LEAD + r * SLOTS + before)
                for b in range(2):
                    for h in range(H):
                        c, i = divmod(h, H // 2)
                        last = pe.matmul(score[g][S * b:S * b + S, c, i * S:(i + 1) * S],
                                         qbd[g][:, c, i, b * S:(b + 1) * S], kT[g][:, c, b * S:(b + 1) * S],
                                         start=True, stop=True)
                last.then_inc(s_sc, 1)

            def turn_probs(r, g):
                pe.wait_ge(s_exp, r * SLOTS + before + g + 1)
                for j in range(NP):
                    last = pe.transpose(score[g][:, j // 4, (j % 4) * P:(j % 4 + 1) * P],
                                        prob[g][:, 2 * j:2 * j + 2, :], ident[:, :])
                last.then_inc(s_pT, 1)

            def values(r, g):
                pe.wait_ge(s_pTa, r * SLOTS + before + g + 1)
                pe.wait_ge(s_pTd, r * SLOTS + before + g + 1)
                for b in range(2):
                    for j in range(NP):
                        last = pe.matmul(score[g][S * b:S * b + S, 0, j * VW:(j + 1) * VW],
                                         probT[g][:, j, b * S:(b + 1) * S], vbd[g][:, b, j, :],
                                         start=True, stop=True)
                last.then_inc(s_o, 1)

            def turn_heads(r, g):
                pe.wait_ge(s_on, r * SLOTS + before + g + 1)
                for c in range(DC):
                    last = pe.transpose(score[g][:, 1, c * P:(c + 1) * P], heads[g][:, c * P:(c + 1) * P], ident[:, :])
                last.then_inc(s_oT, 1)

            def out(r, g):
                pe.wait_ge(s_oTc, r * SLOTS + before + g + 1)
                for c in range(DC):
                    last = pe.matmul(score[g][:, 0, 0:D], headsT[g][:, c, :], w["o"][:, c, :],
                                     start=(c == 0), stop=(c == DC - 1))
                last.then_inc(s_y, 1)

            pe.wait_ge(s_one, 3 * SLOTS * (nth + 1))
            with pe.Fori(0, ROUNDS) as r:
                for stage in (turn_x, project, turn_qk, scores, turn_probs, values, turn_heads, out):
                    for g in G:
                        stage(r, g)

        @block.scalar
        def _(act):
            def keep_xT(r, g):
                act.wait_ge(s_xT, r * SLOTS + before + g + 1)
                act.copy(xnT[g][:, :, :], front[g][:, 0:D]).then_inc(s_xTc, 1)

            def keep_qkv(r, g):
                if kind == "context":
                    act.wait_ge(s_qk, LEAD + r * SLOTS + before + g + 1)
                    act.copy(qk[g][:, :], front[g][:, :]).then_inc(s_qkc, 1)
                if kind != "bias":
                    act.wait_ge(s_v, LEAD + r * SLOTS + before + g + 1)
                    act.wait_ge(s_one, 3 * SLOTS * (nth + 1))
                    v = vps[g][:, :, :].rearrange("p b (j e d) -> p b j e d", e=2, d=DH)
                    act.copy(vbd[g][0:S, :, :, 0:DH], v[0:S, :, :, 0, :])
                    act.copy(vbd[g][S:P, :, :, DH:2 * DH], v[S:P, :, :, 1, :]).then_inc(s_vc, 1)

            def keep_kT(r, g):
                act.wait_ge(s_kT, r * SLOTS + before + g + 1)
                act.copy(kT[g][:, :, :], vps[g][:, 0, :]).then_inc(s_kTc, 1)

            def exps(r, g):
                act.wait_ge(s_shift, r * SLOTS + before + g + 1)
                act.activation(prob[g][:, :, :], prob[g][:, :, :], ACT.Exp, scale=DH ** -0.5).then_inc(s_exp, 1)

            def keep_probT(r, g):
                act.wait_ge(s_pT, r * SLOTS + before + g + 1)
                act.copy(probT[g][:, 0:4, :], score[g][:, 0, :]).then_inc(s_pTa, 1)

            def keep_headsT(r, g):
                act.wait_ge(s_oT, r * SLOTS + before + g + 1)
                act.copy(headsT[g][:, :, :], score[g][:, 1, 0:D]).then_inc(s_oTc, 1)

            with act.Fori(0, ROUNDS) as r:
                for stage in (keep_xT, keep_qkv, keep_kT, exps, keep_probT, keep_headsT):
                    for g in G:
                        stage(r, g)

        @block.vector
        def _(dve):
            step = Steps(dve, s_dve)
            if nth == 0:
                dve.sem_inc(s_x, LEAD)

            def normalise(r, g):
                x = x_all[:, bass.ds(r * SLOTS + g, 1), :]
                step.done(dve.bn_stats(stats[g][:, :], x))
                dve.memset(mv[g][:, 2:3], 0.0)
                step.done(dve.bn_aggr(mv[g][:, 0:2], stats[g][:, :]))
                dve.tensor_scalar(mv[g][:, 1:2], mv[g][:, 1:2], EPS, None, ALU.add).then_inc(s_var, 1)
                dve.wait_ge(s_rstd, r * SLOTS + before + g + 1)
                dve.tensor_scalar(xn[g][:, :], x, mv[g][:, 0:1], rstd[g][:, 0:1], ALU.subtract, ALU.mult)\
                    .then_inc(s_xn, 1)

            def keep_qkv(r, g):
                if kind == "context":
                    return
                dve.wait_ge(s_qk, LEAD + r * SLOTS + before + g + 1)
                if kind == "bias":
                    dve.tensor_tensor(qk[g][:, :], front[g][:, :], w["bqk"][:, :], ALU.add).then_inc(s_qkc, 1)
                    dve.wait_ge(s_v, LEAD + r * SLOTS + before + g + 1)
                    dve.wait_ge(s_one, 3 * SLOTS * (nth + 1))
                    for e in range(2):
                        rows = slice(S * e, S * e + S)
                        for b in range(2):
                            v = vps[g][rows, b, :].rearrange("p (j e d) -> p j e d", e=2, d=DH)[:, :, e, :]
                            bv = w["bv"][rows, :].rearrange("p (j e d) -> p j e d", e=2, d=DH)[:, :, e, :]
                            last = dve.tensor_tensor(vbd[g][rows, b, :, e * DH:(e + 1) * DH], v, bv, ALU.add)
                    last.then_inc(s_vc, 1)
                else:
                    t2p = t2[g][:, :].rearrange("p (n e) -> p n e", e=2)
                    fp = front[g][:, :].rearrange("p (n e) -> p n e", e=2)
                    sn = w["sin"][:, :].rearrange("p (n e) -> p n e", e=2)
                    dve.tensor_tensor(t1[g][:, :], front[g][:, :], w["cos"][:, :], ALU.mult)
                    dve.tensor_tensor(t2p[:, :, 0], fp[:, :, 1], sn[:, :, 0], ALU.mult)
                    step.done(dve.tensor_tensor(t2p[:, :, 1], fp[:, :, 0], sn[:, :, 1], ALU.mult))
                    dve.tensor_tensor(qk[g][:, :], t1[g][:, :], t2[g][:, :], ALU.add).then_inc(s_qkc, 1)

            def spread_q(r, g):
                dve.wait_ge(s_qT, r * SLOTS + before + g + 1)
                for c in range(DC):
                    q = front[g][:, c * P:(c + 1) * P].unsqueeze(1).broadcast_to([P, H // 2, P])
                    m = head_rows[:, :].unsqueeze(2).broadcast_to([P, H // 2, P])
                    last = dve.tensor_tensor(qbd[g][:, c, :, :], q, m, ALU.mult)
                last.then_inc(s_qbd, 1)

            def shift(r, g):
                dve.wait_ge(s_sc, r * SLOTS + before + g + 1)
                sc = score[g][:, :, :].rearrange("p c (i k) -> p (c i) k", k=S)
                step.done(dve.tensor_tensor(prob[g][:, :, :], sc, mask[:, :].unsqueeze(1).broadcast_to([P, H, S]), ALU.add))
                step.done(dve.tensor_reduce(rmax[g][:, :], prob[g][:, :, :], AX.X, ALU.max))
                dve.tensor_tensor(prob[g][:, :, :], prob[g][:, :, :],
                                  rmax[g][:, :].unsqueeze(2).broadcast_to([P, H, S]), ALU.subtract)\
                    .then_inc(s_shift, 1)

            def keep_probT(r, g):
                dve.wait_ge(s_pT, r * SLOTS + before + g + 1)
                dve.tensor_copy(probT[g][:, 4:8, :], score[g][:, 1, :]).then_inc(s_pTd, 1)

            def scale_heads(r, g):
                dve.wait_ge(s_o, r * SLOTS + before + g + 1)
                o = score[g][:, 0, 0:NP * VW].rearrange("p (j v) -> p j v", v=VW)
                rd = rden[g][:, :].rearrange("p (j e) -> p j e", e=2)
                step.done(dve.reciprocal(rd, o[:, :, 2 * DH:VW]))
                dve.tensor_tensor(heads[g][:, :].rearrange("p (j e d) -> p j e d", e=2, d=DH),
                                  o[:, :, 0:2 * DH].rearrange("p j (e d) -> p j e d", d=DH),
                                  rd.unsqueeze(3).broadcast_to([P, NP, 2, DH]), ALU.mult).then_inc(s_on, 1)

            def update_x(r, g):
                dve.wait_ge(s_y, r * SLOTS + before + g + 1)
                x = x_all[:, bass.ds(r * SLOTS + g, 1), :]
                ins = dve.tensor_tensor(x, score[g][:, 0, 0:D].unsqueeze(1), x, ALU.add)
                if kind == "bias":
                    step.done(ins)
                    ins = dve.tensor_tensor(x, x, w["bo"][:, :].unsqueeze(1), ALU.add)
                ins.then_inc(s_x, 1)

            with dve.Fori(0, ROUNDS) as r:
                step.start(r * dve_steps + steps_before)
                for stage in (normalise, keep_qkv, spread_q, shift, keep_probT, scale_heads, update_x):
                    for g in G:
                        stage(r, g)
                assert step.n == dve_steps, step.n
    return steps_before + ROUNDS * dve_steps


CH, CK, CQ = 16, 128, 192
HALF = CQ // 2
CP = CH // 2
QW = CP * S
SKP = 1608
KQ = SKP // 4
KC = 402
NKC = SKP // KC
NKT = -(-SK // P)
NSUM = NKT - 1
PIECES = 16


def absorb_weights(nc, sem, a, wbig, mw, wvo):
    with ExitStack() as prep:
        def psb(nm, shape):
            return prep.enter_context(nc.sbuf_tensor(nm, shape, F32))
        wq = psb("cx_wq", [P, CH, D])
        wkcq = psb("cx_wkcq", [P, CH, CQ])
        wqrT = psb("cx_wqrT", [DCX, CH, 2, CQ])
        wkrT = psb("cx_wkrT", [DCX, CH, DCX])
        wkckv = psb("cx_wkckv", [P, CH, DCX])
        woT = psb("cx_woT", [P, CH, D])
        bank = [prep.enter_context(nc.psum_tensor(f"cx_prep{i}", [P, 512], F32)) for i in range(8)]
        load(nc, sem("cx_prep_loaded"), [
            (wq[:, :, :], a["cx_wq"]), (wkcq[:, :, :], a["cx_wkcq"]), (wqrT[:, :, :, :], a["cx_wqrT"]),
            (wkrT[:, :, :], a["cx_wkrT"]), (wkckv[:, :, :], a["cx_wkckv"]), (woT[:, :, :], a["cx_woT"])])
        s_made = sem("cx_prep_made")
        s_dve = sem("cx_prep_kept_dve")
        s_act = sem("cx_prep_kept_act")

        def big(pe, o, n):
            j, c = divmod(n, DC)
            for e in range(2):
                last = pe.matmul(o[:, e * CQ:(e + 1) * CQ], wq[:, 2 * j + e, c * P:(c + 1) * P],
                                 wkcq[:, 2 * j + e, :], start=True, stop=True)
            return last

        def rotated(pe, o, j):
            for cs in range(2):
                for e, tile, rows, cols in ((0, 0, slice(0, P), slice(0, P)), (0, 1, slice(0, 64), slice(P, CQ)),
                                            (1, 1, slice(64, P), slice(P, CQ)), (1, 2, slice(0, P), slice(0, P))):
                    at = (cs * 3 + tile) * DCX
                    last = pe.matmul(o[rows, at:at + DCX], wqrT[:, 2 * j + e, cs, cols], wkrT[:, 2 * j + e, :],
                                     start=True, stop=True)
            return last

        def values(pe, o, j):
            for e in range(2):
                last = pe.matmul(o[DCX * e:DCX * e + DCX, 0:D], wkckv[:, 2 * j + e, :], woT[:, 2 * j + e, :],
                                 start=True, stop=True)
            return last

        jobs = [(big, n, wbig[:, n % DC, n // DC, :], 2 * CQ) for n in range(CP * DC)]
        jobs += [(rotated, j, mw[:, j, :, :, :], 6 * DCX) for j in range(CP)]
        jobs += [(values, j, wvo[:, j, :], D) for j in range(CP)]
        with nc.Block() as block:

            @block.tensor
            def _(pe):
                for n, (product, j, _, _) in enumerate(jobs):
                    if n >= 8:
                        pe.wait_ge(s_act if n % 2 else s_dve, (n - 8) // 2 + 1)
                    product(pe, bank[n % 8], j).then_inc(s_made, 1)

            @block.vector
            def _(dve):
                for n, (_, _, kept, w) in enumerate(jobs):
                    if n % 2 == 0:
                        dve.wait_ge(s_made, n + 1)
                        dve.tensor_copy(kept, bank[n % 8][:, 0:w]).then_inc(s_dve, 1)

            @block.scalar
            def _(act):
                for n, (_, _, kept, w) in enumerate(jobs):
                    if n % 2 == 1:
                        act.wait_ge(s_made, n + 1)
                        act.copy(kept, bank[n % 8][:, 0:w]).then_inc(s_act, 1)


def context_attention(nc, sb, pb, sem, a, x_all, const):
    ident = const["ident"]
    wbig = sb("cx_wbig", [P, DC, CP, 2 * CQ])
    mw = sb("cx_mw", [P, CP, 2, 3, DCX])
    wvo = sb("cx_wvo", [P, CP, D])
    absorb_weights(nc, sem, a, wbig, mw, wvo)

    tab = sb("cx_tab", [P, 2, 3, S])
    kcos = sb("cx_kcos", [DCX, SKP])
    ksin = sb("cx_ksin", [DCX, SKP])
    ctx = sb("cx_ctx", [DCX, SKP])
    ctxr = sb("cx_ctxr", [DCX, SKP])
    kr = sb("cx_kr", [DCX, SKP])
    k1 = [sb(f"cx_k1{i}", [P, SKP], F32R) for i in range(2)]
    k2 = [sb(f"cx_k2{i}", [P, SKP], F32R) for i in range(2)]
    kv = [sb(f"cx_kv{i}", [P, NKT, DCX]) for i in range(2)]
    q1 = [sb(f"cx_q1{i}", [P, 2, CP, S], F32R) for i in range(2)]
    q2 = [sb(f"cx_q2{i}", [P, 2, CP, S], F32R) for i in range(2)]
    qs = sb("cx_qs", [DCX, 2, CP, S])
    stats = sb("cx_stats", [P, 6])
    mv = sb("cx_mv", [P, 3])
    rstd = sb("cx_rstd", [P, 1])
    xn = sb("cx_xn", [P, D])
    xnT = sb("cx_xnT", [P, DC, P])
    turn = [sb(f"cx_turn{i}", [P, 2, 3, 2, S]) for i in range(2)]
    RING = 3
    prob = [sb(f"cx_prob{i}", [P, 2, QW]) for i in range(RING)]
    acc = [sb(f"cx_acc{e}", [P, QW]) for e in range(2)]
    ones = sb("cx_ones", [P, DCX])
    identb = sb("cx_identb", [P, P], BF16)
    mhalf = sb("cx_mhalf", [P, PIECES // 2, 2])
    nmax = sb("cx_nmax", [P, PIECES // 2])
    nmh = sb("cx_nmh", [P, PIECES // 2], BF16)
    nml = sb("cx_nml", [P, PIECES // 2], BF16)
    rden = sb("cx_rden", [P, QW])
    heads = sb("cx_heads", [P, QW])

    mx = [pb(f"cx_mx{i}", [P, 2, 512]) for i in range(2)]
    st = [pb(f"cx_st{e}", [P, 512]) for e in range(2)]
    av = pb("cx_av", [P, 512])
    misc = pb("cx_misc", [P, 512])

    load(nc, sem("cx_loaded"), [(tab[:, :, :, :], a["cx_tab"]), (kcos[:, :], a["cx_kcos"]),
                                (ksin[:, :], a["cx_ksin"])])

    s_set = sem("cx_padding_set")
    s_one = sem("cx_ones_set")
    s_ctx = sem("cx_context_loaded")
    s_rope = sem("cx_context_turned")
    s_kr = sem("cx_keys_summed")
    s_k1 = sem("cx_kh_kept")
    s_k2 = sem("cx_k2_kept")
    s_kl = sem("cx_kl_kept")
    s_kt = sem("cx_keys_transposed")
    s_kv = sem("cx_kv_kept")
    s_var = sem("cx_variance")
    s_rstd = sem("cx_rstd_made")
    s_xn = sem("cx_normalised")
    s_xT = sem("cx_x_turned")
    s_xTc = sem("cx_xT_kept")
    s_big = sem("cx_big_queries")
    s_rot = sem("cx_queries_rotated")
    s_eff = sem("cx_queries_made")
    s_q1a = sem("cx_even_q1_kept")
    s_q2a = sem("cx_even_q2_kept")
    s_q1b = sem("cx_odd_q1_kept")
    s_q2b = sem("cx_odd_q2_kept")
    s_mx = sem("cx_max_scores")
    s_mr = sem("cx_max_reduced")
    s_nm = sem("cx_negated_max")
    s_row = sem("cx_max_row")
    s_rowk = sem("cx_max_row_kept")
    s_st = sem("cx_scores")
    s_exp = sem("cx_exp")
    s_av = sem("cx_values_added")
    s_acc = [sem("cx_even_sum"), sem("cx_odd_sum")]
    s_sum = sem("cx_denominators")
    s_rcp = sem("cx_reciprocals")
    s_hd = sem("cx_heads_scaled")
    s_out = sem("cx_out")
    s_x = sem("cx_x_updated")
    s_dve = sem("cx_dve_step")

    def nk(kt):
        return min(P, SK - kt * P)

    def pieces(kt):
        first = lambda k: min(max(0, (3 * (k - 2) + 1) // 2), PIECES)
        return range(first(kt), first(kt + 1) if kt < NKT - 1 else PIECES)

    def batches(engine, before, batch):
        before()
        with engine.Fori(0, NT - 1) as t:
            for e in range(2):
                batch(t, 2 * t + e, e, True, True)
        for e in range(2):
            batch(NT - 1, 2 * (NT - 1) + e, e, False, e == 0)


    with nc.Block() as block:

        @block.sync
        def _(sp):
            def fetch(n):
                sp.dma_start(ctx[:, :], a["cx_ctxT"][bass.ds(n, 1), :, :]).then_inc(s_ctx, 16)
                sp.dma_start(ctxr[:, :], a["cx_ctxrT"][bass.ds(n, 1), :, :]).then_inc(s_ctx, 16)

            fetch(0)
            with sp.Fori(1, B) as n:
                sp.wait_ge(s_kr, n * NKC)
                fetch(n)

        @block.gpsimd
        def _(pool):
            pool.sem_inc(s_acc[0], LEAD)

            def rotate(n, c):
                cols = slice(c * KC, (c + 1) * KC)
                if c == 0:
                    pool.wait_ge(s_ctx, 32 * n + 32)
                pool.tensor_tensor(ctx[:, cols], ctx[:, cols], kcos[:, cols], ALU.mult)
                pool.tensor_tensor(ctxr[:, cols], ctxr[:, cols], ksin[:, cols], ALU.mult).then_inc(s_rope, 1)

            def root(t):
                pool.wait_ge(s_var, t + 1)
                pool.tensor_tensor(rstd[:, :], mv[:, 1:2], const["minus_half"][:, 0:1], ALU.pow).then_inc(s_rstd, 1)

            def add(n, kt):
                if kt == 0:
                    return
                rows = slice(0, nk(kt))
                pool.wait_ge(s_exp, LEAD + n * 2 * NKT + 2 * kt + 1)
                if kt == 1:
                    pool.wait_ge(s_sum, LEAD + n)
                else:
                    pool.wait_ge(s_acc[0], LEAD + n * NSUM + kt - 1)
                sofar = prob[0][rows, 0, :] if kt == 1 else acc[0][rows, :]
                pool.tensor_tensor(acc[0][rows, :], sofar, prob[kt % RING][rows, 0, :], ALU.add)\
                    .then_inc(s_acc[0], 1)

            def before():
                for i in range(2):
                    pool.memset(k2[i][DCX:P, :].bitcast(F32), 0.0).then_inc(s_set, 1)
                    pool.memset(q2[i][DCX:P, :, :, :].bitcast(F32), 0.0).then_inc(s_set, 1)
                pool.wait_ge(s_set, 4)
                for i in range(2):
                    pool.memset(k2[i][DCX:DCX + 1, :].bitcast(F32), 1.0).then_inc(s_set, 1)
                pool.wait_ge(s_set, 6)
                root(0)
                for n in range(2):
                    for c in range(NKC):
                        rotate(n, c)

            def batch(t, n, e, follows, next):
                for kt in range(NKT):
                    add(n, kt)
                    if follows and kt % 3 == 2:
                        rotate(n + 2, kt // 3)
                    if follows and e == 0 and kt == NKT - 2:
                        root(t + 1)

            batches(pool, before, batch)

        @block.tensor
        def _(pe):
            for s in (s_av, s_sum, s_st):
                pe.sem_inc(s, LEAD)

            def turn_keys(n, i, q):
                pe.wait_ge(s_kr, (n + 1) * NKC)
                if q == 1:
                    pe.wait_ge(s_kv, 2 * n + 1)
                for kt in range(8 * q, min(8 * q + 8, NKT)):
                    o, keys = misc[0:nk(kt), (kt % 8) * DCX:(kt % 8 + 1) * DCX], kr[:, kt * P:kt * P + nk(kt)]
                    if kt == 8 * q:
                        pe.matmul(o, keys, ident[0:DCX, 0:DCX], start=True, stop=True)
                    else:
                        last = pe.transpose(o, keys, ident[0:DCX, 0:DCX])
                last.then_inc(s_kt, 1)

            def queries(t):
                pe.wait_ge(s_xn, t + 1)
                pe.wait_ge(s_mr, (2 * t) * PIECES)
                for c in range(DC):
                    last = pe.transpose(mx[0][:, 0, c * P:(c + 1) * P], xn[:, c * P:(c + 1) * P], ident[:, :])
                last.then_inc(s_xT, 1)
                pe.wait_ge(s_xTc, t + 1)

                def big(j):
                    if j >= 2:
                        pe.wait_ge(s_rot, t * CP + j - 1)
                    for tile in range(3):
                        for c in range(DC):
                            last = pe.matmul(mx[j % 2][:, 0, tile * P:(tile + 1) * P],
                                             wbig[:, c, j, tile * P:(tile + 1) * P], xnT[:, c, :],
                                             start=(c == 0), stop=(c == DC - 1))
                    last.then_inc(s_big, 1)

                def effective(j):
                    pe.wait_ge(s_rot, t * CP + j + 1)
                    at = (j % 4) * P
                    for cs in range(2):
                        for i in range(2):
                            for e in range(2):
                                tile = (0, 2)[e] if i == 0 else 1
                                rows = slice(0, P) if i == 0 else slice(64 * e, 64 * e + 64)
                                last = pe.matmul(mx[j // 4][DCX * e:DCX * e + DCX, 1, at:at + P],
                                                 mw[rows, j, cs, tile, :], turn[j % 2][rows, cs, tile, :, :],
                                                 start=(cs == 0 and i == 0), stop=(cs == 1 and i == 1))
                    last.then_inc(s_eff, 1)

                for j in range(CP):
                    big(j)
                    if j >= 1:
                        effective(j - 1)
                effective(CP - 1)

            def max_scores(t, n, e, i):
                b = i % 2
                if i == 0:
                    pe.wait_ge(s_kl, n + 1)
                    pe.wait_ge(s_k2, n + 1)
                    if e == 0:
                        pe.wait_ge(s_q1a, 2 * t + 2)
                        pe.wait_ge(s_q2a, 2 * t + 2)
                    else:
                        pe.wait_ge(s_q1b, t + 1)
                        pe.wait_ge(s_q2b, t + 1)
                pe.wait_ge(s_mr, n * PIECES + max(i - 1, 0))
                q = q1[e][:, :, :, :].rearrange("p e j s -> p (e j s)")[:, (i // 2) * P:(i // 2 + 1) * P]
                for h in range(2):
                    lo = (2 * b + h) * KQ
                    last = pe.matmul(mx[b][:, h, 0:KQ], q, k1[e][:, lo:lo + KQ], start=True, stop=True)
                last.then_inc(s_mx, 1)

            def max_rows(n, p, first):
                pe.wait_ge(s_nm, n + 1)
                if first:
                    pe.wait_ge(s_rcp, n)
                else:
                    pe.wait_ge(s_rowk, 2 * n + 1)
                for i in range(4):
                    for part, (w, lo) in enumerate(((nmh, True), (nml, False))):
                        last = pe.matmul(misc[0:1, i * P:(i + 1) * P], w[:, 4 * p + i:4 * p + i + 1], identb[:, :],
                                         start=(part == 0), stop=(part == 1))
                last.then_inc(s_row, 1)

            def scores(n, e, kt):
                keys = slice(kt * P, kt * P + nk(kt))
                for p in range(2):
                    g = 2 * kt + p
                    if g >= 2:
                        pe.wait_ge(s_exp, LEAD + n * 2 * NKT + g - 1)
                    else:
                        pe.wait_ge(s_exp, LEAD + n * 2 * NKT)
                        pe.wait_ge(s_rowk, 2 * n + 2)
                    pe.matmul(st[p][0:nk(kt), :], k1[e][:, keys], q1[e][:, p, :, :], start=True, stop=False)
                    pe.matmul(st[p][0:nk(kt), :], k2[e][:, keys], q2[e][:, p, :, :], start=False, stop=True)\
                        .then_inc(s_st, 1)

            def values(n, e, kt):
                pe.wait_ge(s_exp, LEAD + n * 2 * NKT + 2 * kt + 2)
                if kt == 0:
                    pe.wait_ge(s_kv, 2 * n + 2)
                    pe.wait_ge(s_hd, LEAD + n)
                for p in range(2):
                    last = pe.matmul(av[DCX * p:DCX * p + DCX, :], kv[e][0:nk(kt), kt, :],
                                     prob[kt % RING][0:nk(kt), p, :], start=(kt == 0), stop=(kt == NKT - 1))
                last.then_inc(s_av, 1)

            def denominators(n, next):
                for p in range(2):
                    pe.wait_ge(s_acc[p], LEAD + (n + 1) * NSUM)
                if next:
                    pe.wait_ge(s_kv, 2 * n + 4)
                else:
                    pe.wait_ge(s_x, n)
                for p in range(2):
                    last = pe.matmul(misc[DCX * p:DCX * p + DCX, :], ones[:, :], acc[p][:, :], start=True, stop=True)
                last.then_inc(s_sum, 1)

            def out(n, e, next):
                pe.wait_ge(s_hd, LEAD + n + 1)
                if next:
                    pe.wait_ge(s_rowk, 2 * n + 4)
                for j in range(CP):
                    last = pe.matmul(misc[S * e:S * e + S, 0:D], heads[:, j * S:(j + 1) * S], wvo[:, j, :],
                                     start=(j == 0), stop=(j == CP - 1))
                last.then_inc(s_out, 1)

            def before():
                pe.wait_ge(s_set, 6)
                pe.wait_ge(s_one, 1)
                for n in range(2):
                    if n == 1:
                        pe.wait_ge(s_kv, 2)
                    turn_keys(n, n, 0)
                    turn_keys(n, n, 1)
                queries(0)
                for i in range(PIECES):
                    max_scores(0, 0, 0, i)
                pe.wait_ge(s_kv, 4)
                max_rows(0, 0, True)
                max_rows(0, 1, False)

            def batch(t, n, e, follows, next):
                scores(n, e, 0)
                for kt in range(NKT):
                    if kt + 1 < NKT:
                        scores(n, e, kt + 1)
                    if next:
                        for i in pieces(kt):
                            max_scores(t + e, n + 1, 1 - e, i)
                    values(n, e, kt)
                denominators(n, next)
                if next:
                    max_rows(n + 1, 0, True)
                    max_rows(n + 1, 1, False)
                out(n, e, next)
                if follows:
                    pe.wait_ge(s_x, n + 1)
                    turn_keys(n + 2, e, 0)
                    turn_keys(n + 2, e, 1)
                    if e == 0:
                        queries(t + 1)

            batches(pe, before, batch)

        @block.scalar
        def _(act):
            act.sem_inc(s_exp, LEAD)

            def keep_keys(n, e, later):
                act.wait_ge(s_kr, (n + 1) * NKC)
                if later:
                    act.wait_ge(s_st, LEAD + (n - 1) * 2 * NKT)
                    act.wait_ge(s_mx, (n - 1) * PIECES)
                act.copy(k1[e][0:DCX, :], kr[:, :]).then_inc(s_k1, 1)
                act.copy(k2[e][0:DCX, :], kr[:, :]).then_inc(s_k2, 1)

            def keep_kv(n, e, q, later):
                act.wait_ge(s_kt, 2 * n + q + 1)
                if q == 0 and later:
                    act.wait_ge(s_av, LEAD + (n - 1) * NKT)
                if q == 0:
                    act.copy(kv[e][:, 0:8, :], misc[:, :]).then_inc(s_kv, 1)
                else:
                    m = nk(NKT - 1)
                    act.copy(kv[e][:, 8:NKT - 1, :], misc[:, 0:(NKT - 9) * DCX])
                    act.copy(kv[e][0:m, NKT - 1, :], misc[0:m, (NKT - 9) * DCX:(NKT - 8) * DCX]).then_inc(s_kv, 1)

            def queries(t, later):
                act.wait_ge(s_xT, t + 1)
                act.copy(xnT[:, :, :], mx[0][:, 0, 0:D]).then_inc(s_xTc, 1)
                for g in range(2):
                    act.wait_ge(s_eff, t * CP + 4 * g + 4)
                    if later and g == 0:
                        act.wait_ge(s_st, LEAD + (2 * t - 1) * 2 * NKT)
                        act.wait_ge(s_q2b, t)
                    for e in range(2):
                        q = mx[g][DCX * e:DCX * e + DCX, 1, :].rearrange("p (j b s) -> p j b s", b=2, s=S)
                        for up in range(2):
                            act.copy(q1[0][DCX * up:DCX * up + DCX, e, 4 * g:4 * g + 4, :], q[:, :, 0, :])
                        last = act.copy(qs[:, e, 4 * g:4 * g + 4, :], q[:, :, 1, :])
                    last.then_inc(s_q1a, 1)

            def odd_queries(t, later):
                if later:
                    act.wait_ge(s_st, LEAD + (2 * t) * 2 * NKT)
                for up in range(2):
                    last = act.copy(q1[1][DCX * up:DCX * up + DCX, :, :, :], qs[:, :, :, :])
                last.then_inc(s_q1b, 1)

            def exps(n, kt):
                rows = slice(0, nk(kt))
                for p in range(2):
                    act.wait_ge(s_st, LEAD + n * 2 * NKT + 2 * kt + p + 1)
                    if p == 0:
                        act.wait_ge(s_av, LEAD + n * NKT + max(kt - RING + 1, 0))
                        for s in s_acc:
                            act.wait_ge(s, LEAD + n * NSUM + (max(kt - RING, 1) if kt >= RING else 0))
                    act.activation(prob[kt % RING][rows, p, :], st[p][rows, :], ACT.Exp).then_inc(s_exp, 1)

            def keep_rows(n, e, p):
                act.wait_ge(s_row, 2 * n + p + 1)
                act.copy(q2[e][DCX:DCX + 1, p, :, :], misc[0:1, :]).then_inc(s_rowk, 1)

            def before():
                act.wait_ge(s_set, 6)
                keep_keys(0, 0, False)
                keep_kv(0, 0, 0, False)
                keep_kv(0, 0, 1, False)
                keep_keys(1, 1, False)
                keep_kv(1, 1, 0, False)
                keep_kv(1, 1, 1, False)
                queries(0, False)
                keep_rows(0, 0, 0)
                keep_rows(0, 0, 1)

            def batch(t, n, e, follows, next):
                if e == 0:
                    odd_queries(t, not isinstance(t, int) or t > 0)
                for kt in range(NKT):
                    exps(n, kt)
                if next:
                    keep_rows(n + 1, 1 - e, 0)
                    keep_rows(n + 1, 1 - e, 1)
                if follows:
                    keep_keys(n + 2, e, True)
                    keep_kv(n + 2, e, 0, True)
                    keep_kv(n + 2, e, 1, True)
                    if e == 0:
                        queries(t + 1, True)

            batches(act, before, batch)

        @block.vector
        def _(dve):
            step = Steps(dve, s_dve)
            dve.sem_inc(s_hd, LEAD)
            dve.sem_inc(s_acc[1], LEAD)

            def sum_keys(n, c, later):
                cols = slice(c * KC, (c + 1) * KC)
                dve.wait_ge(s_rope, n * NKC + c + 1)
                if c == 0 and later:
                    dve.wait_ge(s_k2, n)
                    dve.wait_ge(s_kt, 2 * n)
                    dve.wait_ge(s_kl, n)
                dve.tensor_tensor(kr[:, cols], ctx[:, cols], ctxr[:, cols], ALU.add).then_inc(s_kr, 1)

            def keep_kl(n, e):
                dve.wait_ge(s_k1, n + 1)
                dve.wait_ge(s_kr, (n + 1) * NKC)
                dve.tensor_tensor(k1[e][DCX:P, :], kr[:, :], k1[e][0:DCX, :].bitcast(F32), ALU.subtract)\
                    .then_inc(s_kl, 1)

            def normalise(t, base):
                step.start(base)
                x = x_all[:, bass.ds(t, 1), :]
                step.done(dve.bn_stats(stats[:, :], x))
                dve.memset(mv[:, 2:3], 0.0)
                step.done(dve.bn_aggr(mv[:, 0:2], stats[:, :]))
                dve.tensor_scalar(mv[:, 1:2], mv[:, 1:2], EPS, None, ALU.add).then_inc(s_var, 1)
                dve.wait_ge(s_rstd, t + 1)
                dve.tensor_scalar(xn[:, :], x, mv[:, 0:1], rstd[:, 0:1], ALU.subtract, ALU.mult).then_inc(s_xn, 1)

            def queries(t):
                def rotate(j):
                    dve.wait_ge(s_big, t * CP + j + 1)
                    if j >= 2:
                        dve.wait_ge(s_eff, t * CP + j - 1)
                    q = mx[j % 2][:, 0, 0:3 * P].rearrange("p (m b s) -> p m b s", b=2, s=S)
                    for cs in range(2):
                        last = dve.tensor_tensor(turn[j % 2][:, cs, :, :, :], q,
                                                 tab[:, cs, :, :].unsqueeze(2).broadcast_to([P, 3, 2, S]), ALU.mult)
                    last.then_inc(s_rot, 1)

                def split(g):
                    dve.wait_ge(s_q1a, 2 * t + g + 1)
                    for e in range(2):
                        q = mx[g][DCX * e:DCX * e + DCX, 1, :].rearrange("p (j b s) -> p j b s", b=2, s=S)
                        last = dve.tensor_tensor(q2[0][0:DCX, e, 4 * g:4 * g + 4, :], q[:, :, 0, :],
                                                 q1[0][0:DCX, e, 4 * g:4 * g + 4, :].bitcast(F32), ALU.subtract)
                    last.then_inc(s_q2a, 1)

                for j in range(CP):
                    rotate(j)
                    if j == 5:
                        split(0)
                split(1)

            def odd_queries(t):
                dve.wait_ge(s_q1b, t + 1)
                dve.tensor_tensor(q2[1][0:DCX, :, :, :], qs[:, :, :, :], q1[1][0:DCX, :, :, :].bitcast(F32),
                                  ALU.subtract).then_inc(s_q2b, 1)

            def reduce_max(n, i):
                dve.wait_ge(s_mx, n * PIECES + i + 1)
                dve.tensor_reduce(mhalf[:, i // 2, i % 2:i % 2 + 1], mx[i % 2][:, :, 0:KQ], AX.XY, ALU.max)\
                    .then_inc(s_mr, 1)

            def negate_max(n, base):
                step.start(base)
                dve.wait_ge(s_mr, (n + 1) * PIECES)
                step.done(dve.tensor_reduce(nmax[:, :], mhalf[:, :, :], AX.X, ALU.max, negate=True))
                step.done(dve.tensor_copy(nmh[:, :], nmax[:, :]))
                dve.tensor_tensor(nml[:, :], nmax[:, :], nmh[:, :], ALU.subtract).then_inc(s_nm, 1)

            def add(n, kt):
                if kt == 0:
                    return
                rows = slice(0, nk(kt))
                dve.wait_ge(s_exp, LEAD + n * 2 * NKT + 2 * kt + 2)
                if kt == 1:
                    dve.wait_ge(s_sum, LEAD + n)
                else:
                    dve.wait_ge(s_acc[1], LEAD + n * NSUM + kt - 1)
                sofar = prob[0][rows, 1, :] if kt == 1 else acc[1][rows, :]
                dve.tensor_tensor(acc[1][rows, :], sofar, prob[kt % RING][rows, 1, :], ALU.add)\
                    .then_inc(s_acc[1], 1)

            def scale_heads(n):
                dve.wait_ge(s_sum, LEAD + n + 1)
                dve.reciprocal(rden[:, :], misc[:, :]).then_inc(s_rcp, 1)
                dve.wait_ge(s_rcp, n + 1)
                dve.wait_ge(s_av, LEAD + (n + 1) * NKT)
                dve.tensor_tensor(heads[:, :], av[:, :], rden[:, :], ALU.mult).then_inc(s_hd, 1)

            def update_x(t, n, e):
                rows = slice(S * e, S * e + S)
                dve.wait_ge(s_out, n + 1)
                x = x_all[rows, bass.ds(t, 1), :]
                dve.tensor_tensor(x, misc[rows, 0:D].unsqueeze(1), x, ALU.add).then_inc(s_x, 1)

            def before():
                dve.memset(ones[:, :], 1.0)
                dve.tensor_copy(identb[:, :], ident[:, :]).then_inc(s_one, 1)
                normalise(0, 0)
                for n in range(2):
                    for c in range(NKC):
                        sum_keys(n, c, n > 0)
                    keep_kl(n, n)
                queries(0)
                for i in range(PIECES):
                    reduce_max(0, i)
                negate_max(0, 2)

            def batch(t, n, e, follows, next):
                if e == 0:
                    odd_queries(t)
                base = 4 + 6 * t + (4 if e else 0)
                for kt in range(NKT):
                    if next:
                        for i in pieces(kt):
                            reduce_max(n + 1, i)
                    add(n, kt)
                    if follows and kt % 3 == 0 and kt:
                        sum_keys(n + 2, kt // 3 - 1, True)
                    if follows and e == 0 and kt == NKT - 2:
                        normalise(t + 1, base)
                if next:
                    negate_max(n + 1, base + (2 if e == 0 and follows else 0))
                scale_heads(n)
                update_x(t, n, e)
                if follows:
                    keep_kl(n + 2, e)
                    if e == 0:
                        queries(t + 1)

            batches(dve, before, batch)


def context_layout(inp, a, rows, spread):
    f = np.float32
    a["cx_wq"] = inp["L1_xattn_Wq"].reshape(CH, CK, D).transpose(1, 0, 2)
    odd = np.concatenate([np.arange(P, CQ), np.arange(P)])
    wkcq = inp["L1_xattn_w_kc_q"].transpose(1, 0, 2)
    a["cx_wkcq"] = np.stack([wkcq[:, 0::2], wkcq[:, 1::2][:, :, odd]], axis=2).reshape(CK, CH, CQ)
    wqr = inp["L1_xattn_W_qr"]
    a["cx_wqrT"] = np.stack([wqr, np.roll(wqr, HALF, axis=1)], axis=1).transpose(3, 0, 1, 2)
    a["cx_wkrT"] = inp["L1_xattn_W_kr"].transpose(2, 0, 1)
    a["cx_wkckv"] = inp["L1_xattn_w_kc_kv"].transpose(1, 0, 2)
    a["cx_woT"] = inp["L1_xattn_Wo"].reshape(D, CH, CK).transpose(2, 1, 0)

    def angles(n, dim):
        inv = f(1.0) / f(10000.0) ** (np.arange(0, dim, 2, dtype=f) / f(dim))
        g = np.arange(n, dtype=f)[:, None] * inv[None, :].astype(f)
        return np.repeat(np.cos(g), 2, axis=1).astype(f), np.repeat(np.sin(g), 2, axis=1).astype(f)

    cos, sin = angles(S, CQ)
    sin = np.roll(sin, HALF, axis=1) * np.where(np.arange(CQ) < HALF, 1.0, -1.0).astype(f)
    tab = np.stack([cos.T, sin.T], axis=0)
    lo, hi = tab[:, 0:P], tab[:, P:CQ]
    a["cx_tab"] = np.stack([lo, np.concatenate([hi, hi], axis=1), lo], axis=2).transpose(1, 0, 2, 3)
    cos, sin = angles(SK, DCX)
    sin = sin * np.where(np.arange(DCX) < DCX // 2, -1.0, 1.0).astype(f)
    at = np.minimum(np.arange(SKP), SK - 1)
    a["cx_kcos"], a["cx_ksin"] = cos[at].T, sin[at].T
    ctxT = inp["ctx_512"][:, at, :].transpose(0, 2, 1)
    a["cx_ctxT"] = ctxT
    a["cx_ctxrT"] = np.roll(ctxT, DCX // 2, axis=1)


def quantise_rows(dve, step, rows, q_out, amax, inv, back, tmp):
    step.done(dve.tensor_reduce(amax, rows, AX.X, ALU.max, apply_absolute_value=True))
    step.done(dve.tensor_scalar(amax, amax, 1e-5, None, ALU.max))
    dve.tensor_scalar(back, amax, 1.0 / 127.0, None, ALU.mult)
    step.done(dve.reciprocal(inv, amax))
    step.done(dve.tensor_scalar(inv, inv, 127.0, None, ALU.mult))
    step.done(dve.tensor_scalar(tmp, rows, inv, ROUND, ALU.mult, ALU.add))
    step.done(dve.tensor_scalar(tmp, tmp, ROUND, 127.0, ALU.subtract, ALU.min))
    return dve.tensor_scalar(q_out, tmp, -128.0, None, ALU.max)


def quantised_mlp(nc, sb, pb, sem, a, x_all, const):
    ident = const["ident"]
    name = "f0"
    G = range(SLOTS)
    FC = FF // P
    w1T = sb("f0_w1T", [P, DC, FF], BF16)
    w2T = sb("f0_w2T", [P, FC, D], BF16)
    s1row = sb("f0_s1row", [P, FF])
    s2row = sb("f0_s2row", [P, D])
    identb = sb("f0_identb", [P, P], BF16)

    with ExitStack() as prep:
        def psb(nm, shape, dt=F32):
            return prep.enter_context(nc.sbuf_tensor(nm, shape, dt))

        def ppb(nm, shape, dt=F32):
            return prep.enter_context(nc.psum_tensor(nm, shape, dt))
        w1 = psb("f0_w1", [P, FC, D])
        w2 = psb("f0_w2", [P, DC, FF])
        asum = psb("f0_asum", [P, FC + DC])
        rec = psb("f0_rec", [P, FC + DC])
        q1 = psb("f0_q1", [P, FC, D], BF16)
        q2 = psb("f0_q2", [P, DC, FF], BF16)
        diag = psb("f0_diag", [P, FC + DC, P])
        ones = psb("f0_ones", [P, P])
        w1ps = ppb("f0_w1ps", [P, DC, FF], BF16)
        w2ps = ppb("f0_w2ps", [P, FC, D], BF16)
        s1ps = ppb("f0_s1ps", [P, FF])
        s2ps = ppb("f0_s2ps", [P, D])
        load(nc, sem("f0_loaded"), [(w1[:, :, :], a["f0_w1"]), (w2[:, :, :], a["f0_w2"])])
        s_step = sem("f0_prep_step")
        s_q1 = sem("f0_w_quantised")
        s_ps = sem("f0_w_turned")
        with nc.Block() as block:

            @block.vector
            def _(dve):
                step = Steps(dve, s_step)
                dve.memset(ones[:, :], 1.0)
                dve.tensor_copy(identb[:, :], ident[:, :])
                for w, q, lo, n, width in ((w1, q1, 0, FC, D), (w2, q2, FC, DC, FF)):
                    sc, rc = asum[:, lo:lo + n], rec[:, lo:lo + n]
                    step.done(dve.tensor_reduce(sc, w[:, :, :], AX.X, ALU.add, apply_absolute_value=True))
                    step.done(dve.tensor_scalar(sc, sc, 1.0 / width, 1e-5, ALU.mult, ALU.max))
                    step.done(dve.reciprocal(rc, sc))
                    step.done(dve.tensor_tensor(w[:, :, :], w[:, :, :], rc.unsqueeze(2).broadcast_to([P, n, width]),
                                                ALU.mult))
                    step.done(dve.tensor_scalar(w[:, :, :], w[:, :, :], ROUND, ROUND, ALU.add, ALU.subtract))
                    step.done(dve.tensor_scalar(q[:, :, :], w[:, :, :], 1.0, -1.0, ALU.min, ALU.max))
                    for i in range(n):
                        last = dve.tensor_scalar(diag[:, lo + i, :], ident[:, :], asum[:, lo + i:lo + i + 1], None,
                                                 ALU.mult)
                last.then_inc(s_q1, 1)
                dve.wait_ge(s_ps, 1)
                dve.tensor_copy(w1T[:, :, :], w1ps[:, :, :])
                dve.tensor_copy(w2T[:, :, :], w2ps[:, :, :])
                dve.tensor_copy(s1row[:, :], s1ps[:, :])
                dve.tensor_copy(s2row[:, :], s2ps[:, :]).then_inc(s_step, 1)

            @block.tensor
            def _(pe):
                pe.wait_ge(s_q1, 1)
                for i in range(FC):
                    for c in range(DC):
                        pe.transpose(w1ps[:, c, i * P:(i + 1) * P], q1[:, i, c * P:(c + 1) * P], identb[:, :])
                        pe.transpose(w2ps[:, i, c * P:(c + 1) * P], q2[:, c, i * P:(i + 1) * P], identb[:, :])
                for i in range(FC):
                    pe.matmul(s1ps[:, i * P:(i + 1) * P], ones[:, :], diag[:, i, :], start=True, stop=True)
                for i in range(DC):
                    last = pe.matmul(s2ps[:, i * P:(i + 1) * P], ones[:, :], diag[:, FC + i, :], start=True, stop=True)
                last.then_inc(s_ps, 1)

    stats = [sb(f"{name}_stats{g}", [P, 6]) for g in G]
    mv = [sb(f"{name}_mv{g}", [P, 3]) for g in G]
    rstd = [sb(f"{name}_rstd{g}", [P, 1]) for g in G]
    xn = [sb(f"{name}_xn{g}", [P, D]) for g in G]
    amax = [sb(f"{name}_amax{g}", [P, 2]) for g in G]
    inv = [sb(f"{name}_inv{g}", [P, 2]) for g in G]
    back = [sb(f"{name}_back{g}", [P, 2]) for g in G]
    y1 = [sb(f"{name}_y1{g}", [P, D], BF16) for g in G]
    y1T = [sb(f"{name}_y1T{g}", [P, DC, P], BF16) for g in G]
    hid = [sb(f"{name}_hid{g}", [P, FF]) for g in G]
    tmp = [sb(f"{name}_tmp{g}", [P, FF]) for g in G]
    y2 = [sb(f"{name}_y2{g}", [P, FF], BF16) for g in G]
    y2T = [sb(f"{name}_y2T{g}", [P, FC, P], BF16) for g in G]
    front = [pb(f"{name}_front{g}", [P, 512]) for g in G]
    up = [pb(f"{name}_up{g}", [P, FF]) for g in G]
    turned = [pb(f"{name}_turned{g}", [P, FC, P], BF16) for g in G]

    s_var = sem("f0_variance")
    s_rstd = sem("f0_rstd")
    s_y1 = sem("f0_y1_quantised")
    s_y1T = sem("f0_y1_turned")
    s_y1Tc = sem("f0_y1T_kept")
    s_up = sem("f0_up")
    s_hid = sem("f0_hidden")
    s_gelu = sem("f0_gelu")
    s_y2 = sem("f0_y2_quantised")
    s_y2T = sem("f0_y2_turned")
    s_y2Tc = sem("f0_y2T_kept")
    s_down = sem("f0_down")
    s_x = sem("f0_x_updated")
    s_dve = sem("f0_dve_step")
    dve_steps = SLOTS * 16

    with nc.Block() as block:

        @block.gpsimd
        def _(pool):
            with pool.Fori(0, ROUNDS) as r:
                for g in G:
                    pool.wait_ge(s_var, r * SLOTS + g + 1)
                    pool.tensor_tensor(rstd[g][:, :], mv[g][:, 1:2], const["minus_half"][:, 0:1], ALU.pow)\
                        .then_inc(s_rstd, 1)

        @block.tensor
        def _(pe):
            def turn_y1(r, g):
                pe.wait_ge(s_y1, r * SLOTS + g + 1)
                pe.wait_ge(s_x, LEAD + r * SLOTS)
                for c in range(DC):
                    last = pe.transpose(front[g][:, c * 64:(c + 1) * 64].bitcast(BF16), y1[g][:, c * P:(c + 1) * P],
                                        identb[:, :])
                last.then_inc(s_y1T, 1)

            def up_product(r, g):
                pe.wait_ge(s_y1Tc, r * SLOTS + g + 1)
                for n in range(2):
                    for c in range(DC):
                        last = pe.matmul(up[g][:, n * 512:(n + 1) * 512], y1T[g][:, c, :],
                                         w1T[:, c, n * 512:(n + 1) * 512], start=(c == 0), stop=(c == DC - 1))
                last.then_inc(s_up, 1)

            def turn_y2(r, g):
                pe.wait_ge(s_y2, r * SLOTS + g + 1)
                for i in range(FC):
                    last = pe.transpose(turned[g][:, i, :], y2[g][:, i * P:(i + 1) * P], identb[:, :])
                last.then_inc(s_y2T, 1)

            def down_product(r, g):
                pe.wait_ge(s_y2Tc, r * SLOTS + g + 1)
                for i in range(FC):
                    last = pe.matmul(front[g][:, 0:D], y2T[g][:, i, :], w2T[:, i, :], start=(i == 0), stop=(i == FC - 1))
                last.then_inc(s_down, 1)

            with pe.Fori(0, ROUNDS) as r:
                for stage in (turn_y1, up_product, turn_y2, down_product):
                    for g in G:
                        stage(r, g)

        @block.scalar
        def _(act):
            def keep_y1T(r, g):
                act.wait_ge(s_y1T, r * SLOTS + g + 1)
                act.copy(y1T[g][:, :, :], front[g][:, 0:P].bitcast(BF16)).then_inc(s_y1Tc, 1)

            def gelu(r, g):
                act.wait_ge(s_hid, r * SLOTS + g + 1)
                act.activation(hid[g][:, :], hid[g][:, :], ACT.Gelu_apprx_tanh).then_inc(s_gelu, 1)

            def keep_y2T(r, g):
                act.wait_ge(s_y2T, r * SLOTS + g + 1)
                act.copy(y2T[g][:, :, :], turned[g][:, :, :]).then_inc(s_y2Tc, 1)

            with act.Fori(0, ROUNDS) as r:
                for stage in (keep_y1T, gelu, keep_y2T):
                    for g in G:
                        stage(r, g)

        @block.vector
        def _(dve):
            step = Steps(dve, s_dve)
            dve.sem_inc(s_x, LEAD)

            def normalise(r, g):
                x = x_all[:, bass.ds(r * SLOTS + g, 1), :]
                step.done(dve.bn_stats(stats[g][:, :], x))
                dve.memset(mv[g][:, 2:3], 0.0)
                step.done(dve.bn_aggr(mv[g][:, 0:2], stats[g][:, :]))
                dve.tensor_scalar(mv[g][:, 1:2], mv[g][:, 1:2], EPS, None, ALU.add).then_inc(s_var, 1)
                dve.wait_ge(s_rstd, r * SLOTS + g + 1)
                step.done(dve.tensor_scalar(xn[g][:, :], x, mv[g][:, 0:1], rstd[g][:, 0:1], ALU.subtract, ALU.mult))
                quantise_rows(dve, step, xn[g][:, :], y1[g][:, :], amax[g][:, 0:1], inv[g][:, 0:1], back[g][:, 0:1],
                              tmp[g][:, 0:D]).then_inc(s_y1, 1)

            def hidden(r, g):
                dve.wait_ge(s_up, r * SLOTS + g + 1)
                dve.scalar_tensor_tensor(out=hid[g][:, :], in0=up[g][:, :], scalar=back[g][:, 0:1], in1=s1row[:, :],
                                         op0=ALU.mult, op1=ALU.mult).then_inc(s_hid, 1)

            def quantise_hidden(r, g):
                dve.wait_ge(s_gelu, r * SLOTS + g + 1)
                quantise_rows(dve, step, hid[g][:, :], y2[g][:, :], amax[g][:, 1:2], inv[g][:, 1:2], back[g][:, 1:2],
                              tmp[g][:, :]).then_inc(s_y2, 1)

            def update_x(r, g):
                dve.wait_ge(s_down, r * SLOTS + g + 1)
                x = x_all[:, bass.ds(r * SLOTS + g, 1), :]
                step.done(dve.scalar_tensor_tensor(out=tmp[g][:, 0:D], in0=front[g][:, 0:D], scalar=back[g][:, 1:2],
                                                   in1=s2row[:, :], op0=ALU.mult, op1=ALU.mult))
                dve.tensor_tensor(x, tmp[g][:, 0:D].unsqueeze(1), x, ALU.add).then_inc(s_x, 1)

            with dve.Fori(0, ROUNDS) as r:
                step.start(r * dve_steps)
                for stage in (normalise, hidden, quantise_hidden, update_x):
                    for g in G:
                        stage(r, g)
                assert step.n == dve_steps, step.n


E, TOPK, FE = 16, 4, 176
NE = 20
NF = NE * FE
NFC = -(-NF // P)


def experts_mlp(nc, sb, pb, sem, a, x_all, const):
    ident = const["ident"]
    G = range(SLOTS)
    wgu = sb("moe_wgu", [P, NE, DC, 2 * FE])
    wd = sb("moe_wd", [P, NFC, D])
    wr = sb("moe_wr", [P, DC, E + 1])
    before = sb("moe_before", [P, E, E])
    stats = [sb(f"moe_stats{g}", [P, 6]) for g in G]
    mv = [sb(f"moe_mv{g}", [P, 3]) for g in G]
    rstd = [sb(f"moe_rstd{g}", [P, 1]) for g in G]
    xn = [sb(f"moe_xn{g}", [P, D]) for g in G]
    xnT = [sb(f"moe_xnT{g}", [P, DC, P]) for g in G]
    logit = [sb(f"moe_logit{g}", [P, E + 1]) for g in G]
    nmax = [sb(f"moe_nmax{g}", [P, 1]) for g in G]
    rw = [sb(f"moe_rw{g}", [P, E + 1]) for g in G]
    rsum = [sb(f"moe_rsum{g}", [P, 1]) for g in G]
    ahead = [sb(f"moe_ahead{g}", [P, E, E]) for g in G]
    equal = [sb(f"moe_equal{g}", [P, E, E]) for g in G]
    rank = [sb(f"moe_rank{g}", [P, E]) for g in G]
    coef = [sb(f"moe_coef{g}", [P, E + 1]) for g in G]
    RING = 3
    silu = [sb(f"moe_silu{i}", [P, FE]) for i in range(RING)]
    hid = sb("moe_hid", [P, NF])
    hidT = [sb(f"moe_hidT{i}", [P, 4, P]) for i in range(2)]
    gu = [pb(f"moe_gu{i}", [P, 512]) for i in range(RING)]
    turned = [pb(f"moe_turned{i}", [P, 4, P]) for i in range(2)]
    front = pb("moe_front", [P, 512])
    acc = pb("moe_acc", [P, 512])

    loaded = sem("moe_loaded")
    pairs = [(wr[:, :, :], a["moe_wr"]), (before[:, :, :], a["moe_before"])]
    pairs += [(wgu[:, 4 * i:4 * i + 4], a["moe_wgu"][:, 4 * i:4 * i + 4]) for i in range(NE // 4)]
    pairs += [(wd[:, 7 * i:7 * i + 7, :], a["moe_wd"][:, 7 * i:7 * i + 7, :]) for i in range(NFC // 7)]
    load(nc, loaded, pairs)

    NQ = NFC // 4
    LAST = [min(-(-(512 * (q + 1)) // FE), NE) - 1 for q in range(NQ)]
    TURN = {min(LAST[q] + 2, NE): q for q in range(NQ)}
    s_var = sem("moe_variance")
    s_rstd = sem("moe_rstd")
    s_xn = sem("moe_normalised")
    s_xT = sem("moe_x_turned")
    s_xTc = sem("moe_xT_kept")
    s_rl = sem("moe_router_logits")
    s_lg = sem("moe_logits_kept")
    s_rx = sem("moe_router_exp")
    s_cf = sem("moe_coefficients")
    s_gu = sem("moe_gate_up")
    s_silu = sem("moe_silu_done")
    s_hid = sem("moe_hidden")
    s_turn = sem("moe_hidden_turned")
    s_turnc = sem("moe_hiddenT_kept")
    s_acc = sem("moe_down")
    s_x = sem("moe_x_updated")
    s_dve = sem("moe_dve_step")
    FRONT_STEPS = 9

    def rounds(engine, tile):
        with engine.Fori(0, ROUNDS - 1) as r:
            for g in G:
                tile(r * SLOTS + g, g, True)
        for g in G:
            tile((ROUNDS - 1) * SLOTS + g, g, g + 1 < SLOTS)

    with nc.Block() as block:

        @block.gpsimd
        def _(pool):
            def root(t, g):
                pool.wait_ge(s_var, t + 1)
                pool.tensor_tensor(rstd[g][:, :], mv[g][:, 1:2], const["minus_half"][:, 0:1], ALU.pow)\
                    .then_inc(s_rstd, 1)

            def tile(t, g, follows):
                if follows:
                    root(t + 1, 1 - g)

            root(0, 0)
            rounds(pool, tile)

        @block.tensor
        def _(pe):
            pe.sem_inc(s_turn, LEAD)

            def turn_x(t, g):
                pe.wait_ge(s_xn, t + 1)
                for c in range(DC):
                    last = pe.transpose(front[:, c * P:(c + 1) * P], xn[g][:, c * P:(c + 1) * P], ident[:, :])
                last.then_inc(s_xT, 1)

            def router(t, g):
                pe.wait_ge(s_xTc, t + 1)
                for c in range(DC):
                    last = pe.matmul(front[:, 0:E + 1], xnT[g][:, c, :], wr[:, c, :],
                                     start=(c == 0), stop=(c == DC - 1))
                last.then_inc(s_rl, 1)

            def gate_up(t, g, e):
                if e >= RING:
                    pe.wait_ge(s_hid, LEAD + t * NE + e - RING + 1)
                else:
                    pe.wait_ge(s_hid, LEAD + t * NE)
                i = e % RING
                for c in range(DC):
                    last = pe.matmul(gu[i][:, 0:2 * FE], xnT[g][:, c, :], wgu[:, e, c, :],
                                     start=(c == 0), stop=(c == DC - 1))
                last.then_inc(s_gu, 1)

            def turn(t, q):
                pe.wait_ge(s_hid, LEAD + t * NE + LAST[q] + 1)
                if q >= 2:
                    pe.wait_ge(s_turnc, LEAD + t * NQ + q - 1)
                else:
                    pe.wait_ge(s_turnc, LEAD + t * NQ)
                for k in range(4 * q, 4 * q + 4):
                    n = min(P, NF - k * P)
                    last = pe.transpose(turned[q % 2][0:n, k % 4, :], hid[:, k * P:k * P + n], ident[:, :])
                last.then_inc(s_turn, 1)

            def down(t, q):
                pe.wait_ge(s_turnc, LEAD + t * NQ + q + 1)
                if q == 0:
                    pe.wait_ge(s_x, LEAD + t)
                for k in range(4 * q, 4 * q + 4):
                    n = min(P, NF - k * P)
                    last = pe.matmul(acc[:, 0:D], hidT[q % 2][0:n, k % 4, :], wd[0:n, k, :],
                                     start=(k == 0), stop=(k == NFC - 1))
                if q == NQ - 1:
                    last.then_inc(s_acc, 1)

            def tile(t, g, follows):
                for e in range(NE):
                    gate_up(t, g, e)
                    if e in TURN:
                        turn(t, TURN[e])
                        if TURN[e] >= 1:
                            down(t, TURN[e] - 1)
                if follows:
                    turn_x(t + 1, 1 - g)
                turn(t, NQ - 1)
                down(t, NQ - 2)
                if follows:
                    router(t + 1, 1 - g)
                down(t, NQ - 1)

            turn_x(0, 0)
            router(0, 0)
            rounds(pe, tile)

        @block.scalar
        def _(act):
            act.sem_inc(s_turnc, LEAD)

            def keep_xT(t, g):
                act.wait_ge(s_xT, t + 1)
                act.copy(xnT[g][:, :, :], front[:, 0:D]).then_inc(s_xTc, 1)

            def router_exp(t, g):
                act.wait_ge(s_lg, t + 1)
                act.activation(rw[g][:, 0:E], logit[g][:, 0:E], ACT.Exp, bias=nmax[g][:, 0:1],
                               accum_out=rsum[g][:, 0:1])
                act.activation(rw[g][:, E:E + 1], logit[g][:, E:E + 1], ACT.Exp, scale=-1.0).then_inc(s_rx, 1)

            def silus(t, e):
                act.wait_ge(s_gu, t * NE + e + 1)
                act.activation(silu[e % RING][:, :], gu[e % RING][:, 0:FE], ACT.Silu).then_inc(s_silu, 1)

            def tile(t, g, follows):
                for e in range(NE):
                    silus(t, e)
                    if e in TURN:
                        keep(t, TURN[e])
                if follows:
                    keep_xT(t + 1, 1 - g)
                keep(t, NQ - 1)
                if follows:
                    router_exp(t + 1, 1 - g)

            def keep(t, q):
                act.wait_ge(s_turn, LEAD + t * NQ + q + 1)
                whole = [k for k in range(4) if (4 * q + k + 1) * P <= NF]
                last = act.copy(hidT[q % 2][:, 0:len(whole), :], turned[q % 2][:, 0:len(whole), :])
                if len(whole) < 4:
                    m = NF % P
                    last = act.copy(hidT[q % 2][0:m, 3, :], turned[q % 2][0:m, 3, :])
                last.then_inc(s_turnc, 1)

            keep_xT(0, 0)
            router_exp(0, 0)
            rounds(act, tile)

        @block.vector
        def _(dve):
            step = Steps(dve, s_dve)
            dve.sem_inc(s_hid, LEAD)
            dve.sem_inc(s_x, LEAD)

            def normalise(t, g):
                x = x_all[:, bass.ds(t, 1), :]
                step.done(dve.bn_stats(stats[g][:, :], x))
                dve.memset(mv[g][:, 2:3], 0.0)
                step.done(dve.bn_aggr(mv[g][:, 0:2], stats[g][:, :]))
                dve.tensor_scalar(mv[g][:, 1:2], mv[g][:, 1:2], EPS, None, ALU.add).then_inc(s_var, 1)
                dve.wait_ge(s_rstd, t + 1)
                dve.tensor_scalar(xn[g][:, :], x, mv[g][:, 0:1], rstd[g][:, 0:1], ALU.subtract, ALU.mult)\
                    .then_inc(s_xn, 1)

            def logits(t, g):
                dve.wait_ge(s_rl, t + 1)
                step.done(dve.tensor_copy(logit[g][:, :], front[:, 0:E + 1]))
                dve.tensor_reduce(nmax[g][:, :], logit[g][:, 0:E], AX.X, ALU.max, negate=True).then_inc(s_lg, 1)

            def coefficients(t, g):
                dve.wait_ge(s_rx, t + 1)
                dve.tensor_scalar(rw[g][:, E:E + 1], rw[g][:, E:E + 1], 1.0, None, ALU.add)
                step.done(dve.reciprocal(rsum[g][:, :], rsum[g][:, :]))
                dve.reciprocal(coef[g][:, E:E + 1], rw[g][:, E:E + 1])
                step.done(dve.tensor_scalar(rw[g][:, 0:E], rw[g][:, 0:E], rsum[g][:, 0:1], None, ALU.mult))
                other = rw[g][:, 0:E].unsqueeze(1).broadcast_to([P, E, E])
                own = rw[g][:, 0:E].unsqueeze(2).broadcast_to([P, E, E])
                step.done(dve.tensor_tensor(equal[g][:, :, :], other, own, ALU.is_equal))
                dve.tensor_tensor(ahead[g][:, :, :], other, own, ALU.is_gt)
                step.done(dve.tensor_tensor(equal[g][:, :, :], equal[g][:, :, :], before[:, :, :], ALU.mult))
                step.done(dve.tensor_tensor(ahead[g][:, :, :], ahead[g][:, :, :], equal[g][:, :, :], ALU.add))
                step.done(dve.tensor_reduce(rank[g][:, :], ahead[g][:, :, :], AX.X, ALU.add))
                dve.scalar_tensor_tensor(out=coef[g][:, 0:E], in0=rank[g][:, :], scalar=float(TOPK), in1=rw[g][:, 0:E],
                                         op0=ALU.is_lt, op1=ALU.mult).then_inc(s_cf, 1)

            def hidden(t, g, e):
                dve.wait_ge(s_silu, t * NE + e + 1)
                k = min(e, E)
                if e == 0:
                    dve.wait_ge(s_cf, t + 1)
                    dve.wait_ge(s_turn, LEAD + t * NQ)
                dve.scalar_tensor_tensor(out=hid[:, e * FE:(e + 1) * FE], in0=silu[e % RING][:, :],
                                         scalar=coef[g][:, k:k + 1], in1=gu[e % RING][:, FE:2 * FE],
                                         op0=ALU.mult, op1=ALU.mult).then_inc(s_hid, 1)

            def update_x(t):
                dve.wait_ge(s_acc, t + 1)
                x = x_all[:, bass.ds(t, 1), :]
                dve.tensor_tensor(x, acc[:, 0:D].unsqueeze(1), x, ALU.add).then_inc(s_x, 1)

            def tile(t, g, follows):
                for e in range(NE):
                    hidden(t, g, e)
                    if e == NE // 2 and follows:
                        step.start(t * FRONT_STEPS + FRONT_STEPS)
                        normalise(t + 1, 1 - g)
                if follows:
                    logits(t + 1, 1 - g)
                    coefficients(t + 1, 1 - g)
                    assert step.n == FRONT_STEPS, step.n
                update_x(t)

            normalise(0, 0)
            logits(0, 0)
            coefficients(0, 0)
            rounds(dve, tile)


def more_layout(inp, a, rows, spread):
    context_layout(inp, a, rows, spread)
    f = np.float32
    a["f0_w1"] = inp["L0_ffn_w1"].reshape(FF // P, P, D).transpose(1, 0, 2)
    a["f0_w2"] = inp["L0_ffn_w2"].reshape(D // P, P, FF).transpose(1, 0, 2)
    a["moe_wr"] = rows(np.concatenate([inp["L1_ffn_gate_w"], inp["L1_ffn_sgate_w"]], axis=0))
    j, e = np.arange(E)[None, :], np.arange(E)[:, None]
    a["moe_before"] = spread((j < e).astype(f))
    sgu = inp["L1_ffn_shared_gate_up_w"].reshape(2, NE - E, FE, D).transpose(1, 0, 2, 3).reshape(NE - E, 2 * FE, D)
    wgu = np.concatenate([inp["L1_ffn_w13"], sgu], axis=0)
    a["moe_wgu"] = wgu.reshape(NE, 2 * FE, DC, P).transpose(3, 0, 2, 1)
    wd = np.concatenate([inp["L1_ffn_w2"].transpose(0, 2, 1).reshape(E * FE, D), inp["L1_ffn_shared_down_w"].T,
                         np.zeros((NFC * P - NF, D), f)], axis=0)
    a["moe_wd"] = wd.reshape(NFC, P, D).transpose(1, 0, 2)


def load(nc, sem_loaded, pairs):
    n = len(pairs)
    with nc.Block() as block:

        @block.sync
        def _(sp):
            for dst, src in pairs[0::2]:
                sp.dma_start(dst, src).then_inc(sem_loaded, 16)
            sp.wait_ge(sem_loaded, 16 * n)

        @block.scalar
        def _(act):
            for dst, src in pairs[1::2]:
                act.dma_start(dst, src).then_inc(sem_loaded, 16)


def perceiver(nc, a, out):
    with ExitStack() as whole:
        semaphores = {}

        def sem(name):
            if name not in semaphores:
                semaphores[name] = whole.enter_context(nc.semaphore(name))
            return semaphores[name]

        def holder(stack):
            def sb(name, shape, dt=F32):
                return stack.enter_context(nc.sbuf_tensor(name, shape, dt))

            def pb(name, shape, dt=F32):
                return stack.enter_context(nc.psum_tensor(name, shape, dt))
            return sb, pb

        sb, _ = holder(whole)
        x_all = sb("x_all", [P, NT, D])
        const = {
            "ident": sb("ident", [P, P]),
            "mask": sb("mask", [P, S]),
            "head_rows": sb("head_rows", [P, H // 2]),
            "minus_half": sb("minus_half", [P, 1]),
        }
        pairs = [(x_all[:, :, :], a["x"].rearrange("(t p) d -> p t d", p=P))]
        pairs += [(const[k][:, :], a[k]) for k in const]
        load(nc, sem("s_const_loaded"), pairs)

        nth, steps = 0, 0
        for phase in PHASES:
            with ExitStack() as stack:
                sb, pb = holder(stack)
                if phase in ("a0", "a1", "a2"):
                    kind = {"a0": "context", "a1": "bias", "a2": "rope"}[phase]
                    w, pairs = {}, []

                    def weight(key, shape):
                        w[key] = sb(f"{phase}_w{key}", shape)
                        dst = w[key][tuple(slice(None) for _ in shape)]
                        pairs.append((dst, a[f"{phase}_{key}"]))
                    if kind == "context":
                        weight("q", [P, DC, D])
                        weight("k", [DCX, D])
                        weight("v", [DCX, D])
                        weight("ctx", [DCX, B * S])
                    else:
                        weight("qk", [P, DC, 2 * D])
                        weight("v", [P, DC, D])
                    weight("o", [P, DC, D])
                    if kind == "bias":
                        weight("bqk", [P, 2 * D])
                        weight("bv", [P, D])
                        weight("bo", [P, D])
                    if kind == "rope":
                        weight("cos", [P, 2 * D])
                        weight("sin", [P, 2 * D])
                    load(nc, sem(f"s_{phase}_loaded"), pairs)
                    steps = small_attention(nc, sb, pb, sem, kind, phase, w, x_all, const, nth, steps)
                    nth += 1
                elif phase == "f0":
                    quantised_mlp(nc, sb, pb, sem, a, x_all, const)
                elif phase == "cx":
                    context_attention(nc, sb, pb, sem, a, x_all, const)
                elif phase == "moe":
                    experts_mlp(nc, sb, pb, sem, a, x_all, const)

        s_out = sem("s_out")
        with nc.Block() as block:

            @block.sync
            def _(sp):
                sp.dma_start(out.rearrange("(t p) d -> p t d", p=P), x_all[:, :, :]).then_inc(s_out, 16)
                sp.wait_ge(s_out, 16)


PHASES = ("a0", "a1", "f0", "cx", "a2", "moe")


def _layout(inp):
    f = np.float32

    def rows(m):
        n, k = m.shape
        return m.T.reshape(k // P, P, n).transpose(1, 0, 2)

    def spread(v):
        return np.broadcast_to(v, (P,) + v.shape)

    a = {"x": inp["x"].reshape(B * S, D)}
    a["ident"] = np.eye(P, dtype=f)
    q, k = np.arange(P)[:, None] % S, np.arange(S)[None, :]
    a["mask"] = np.where(k <= q, 0.0, np.finfo(f).min).astype(f)
    a["head_rows"] = (np.arange(P)[:, None] // DH == np.arange(H // 2)[None, :]).astype(f)
    a["minus_half"] = np.full((P, 1), -0.5, f)

    a["a0_q"] = rows(inp["L0_xattn_Wq"])
    a["a0_k"] = inp["L0_xattn_Wkv_expand"][0:D].T
    a["a0_v"] = inp["L0_xattn_Wkv_expand"][D:].T
    a["a0_ctx"] = inp["ctx_512"][:, 0:S, :].transpose(2, 0, 1).reshape(DCX, B * S)
    a["a0_o"] = rows(inp["L0_xattn_Wout"])
    for ph, src in (("a1", "L0_attn"), ("a2", "L1_attn")):
        a[f"{ph}_qk"] = np.concatenate([rows(inp[f"{src}_Wq"]), rows(inp[f"{src}_Wk"])], axis=2)
        a[f"{ph}_v"] = rows(inp[f"{src}_Wv"])
        a[f"{ph}_o"] = rows(inp[f"{src}_Wo"])
    a["a1_bqk"] = spread(np.concatenate([inp["L0_attn_bq"], inp["L0_attn_bk"]]))
    a["a1_bv"] = spread(inp["L0_attn_bv"])
    a["a1_bo"] = spread(inp["L0_attn_bo"])
    theta = f(10000.0) ** (f(-2.0) * np.arange(DH // 2, dtype=f) / f(DH))
    angle = (np.arange(P) % S).astype(f)[:, None] * theta[None, :].astype(f)
    cos, sin = np.cos(angle).astype(f), np.sin(angle).astype(f)
    a["a2_cos"] = np.tile(np.repeat(cos, 2, axis=1), (1, 2 * H))
    a["a2_sin"] = np.tile(np.stack([-sin, sin], axis=2).reshape(P, DH), (1, 2 * H))
    more_layout(inp, a, rows, spread)
    return {k: np.ascontiguousarray(v) for k, v in a.items()}


def kernel(**inputs):
    import concourse.bacc as bacc
    from concourse.bass_utils import run_bass_kernel_spmd

    nc = bacc.Bacc("TRN2", target_bir_lowering=False, num_devices=1)
    arrays = _layout({k: np.asarray(v) for k, v in inputs.items()})
    aps = {k: nc.dram_tensor(f"in_{k}", v.shape, mybir.dt.from_np(v.dtype), kind="ExternalInput").ap()
           for k, v in arrays.items()}
    out = nc.dram_tensor("out_x", (B * S, D), F32, kind="ExternalOutput").ap()
    perceiver(nc, aps, out)
    r = run_bass_kernel_spmd(nc, [{f"in_{k}": v for k, v in arrays.items()}], core_ids=[0])
    return r.results[0]["out_x"].reshape(B, S, D)
```

```python
import math
from contextlib import ExitStack

import numpy as np

import concourse.bass as bass
from concourse import mybir

F32 = mybir.dt.float32
F32R = mybir.dt.float32r
BF16 = mybir.dt.bfloat16
ALU = mybir.AluOpType
ACT = mybir.ActivationFunctionType
AX = mybir.AxisListType

P = 128
B, S, D = 32, 64, 256
NT = B * S // P
DC = D // P
H, DH = 16, 16
NP = H // 2
SLOTS = 2
ROUNDS = NT // SLOTS
EPS = 1e-5
SK = 1601
DCX = 64
FF = 1024
ROUND = 1.5 * 2.0 ** 23
VW = 2 * DH + 2


LEAD = 1


class Steps:

    def __init__(self, engine, sem):
        self.engine, self.sem, self.base, self.n = engine, sem, 0, 0

    def start(self, base):
        self.base, self.n = base, 0

    def each(self, make):
        for g in range(SLOTS):
            last = make(g)
        self.done(last)

    def done(self, instruction):
        instruction.then_inc(self.sem, 1)
        self.n += 1
        self.engine.wait_ge(self.sem, self.base + self.n)


def rounds(engine, first, order, start=lambda r: None):
    for stage in first:
        for g in range(SLOTS):
            stage(0, g)
    with engine.Fori(0, ROUNDS - 1) as r:
        start(r)
        for stage, ahead in order:
            for g in range(SLOTS):
                stage(r + 1 if ahead else r, g)
    start(ROUNDS - 1)
    for stage, ahead in order:
        for g in range(SLOTS):
            if not ahead:
                stage(ROUNDS - 1, g)


def small_attention(nc, sb, pb, sem, kind, name, w, x_all, const, nth, steps_before):
    ident, mask, head_rows = const["ident"], const["mask"], const["head_rows"]
    G = range(SLOTS)
    before = nth * NT

    stats = [sb(f"{name}_stats{g}", [P, 6]) for g in G]
    mv = [sb(f"{name}_mv{g}", [P, 3]) for g in G]
    rstd = [sb(f"{name}_rstd{g}", [P, 1]) for g in G]
    xn = [sb(f"{name}_xn{g}", [P, D]) for g in G]
    xnT = [sb(f"{name}_xnT{g}", [P, DC, P]) for g in G]
    qk = [sb(f"{name}_qk{g}", [P, 2 * D]) for g in G]
    kT = [sb(f"{name}_kT{g}", [P, DC, P]) for g in G]
    qbd = [sb(f"{name}_qbd{g}", [P, DC, H // 2, P]) for g in G]
    vbd = [sb(f"{name}_vbd{g}", [P, 2, NP, VW]) for g in G]
    prob = [sb(f"{name}_prob{g}", [P, H, S]) for g in G]
    rmax = [sb(f"{name}_rmax{g}", [P, H]) for g in G]
    probT = [sb(f"{name}_probT{g}", [P, NP, P]) for g in G]
    rden = [sb(f"{name}_rden{g}", [P, H]) for g in G]
    heads = [sb(f"{name}_heads{g}", [P, D]) for g in G]
    headsT = [sb(f"{name}_headsT{g}", [P, DC, P]) for g in G]
    front = [pb(f"{name}_front{g}", [P, 512]) for g in G]
    vps = [pb(f"{name}_v{g}", [P, 2, D]) for g in G]
    score = [pb(f"{name}_score{g}", [P, 2, 512]) for g in G]
    if kind == "context":
        ctxT = [sb(f"{name}_ctxT{g}", [DCX, P]) for g in G]
    if kind == "rope":
        t1 = [sb(f"{name}_t1{g}", [P, 2 * D]) for g in G]
        t2 = [sb(f"{name}_t2{g}", [P, 2 * D]) for g in G]

    s_var = sem("attention_variance")
    s_rstd = sem("attention_rstd")
    s_xn = sem("attention_normalised")
    s_xT = sem("attention_x_turned")
    s_xTc = sem("attention_xT_kept")
    s_ctx = sem("attention_ctx_tile")
    s_qk = sem("attention_qk_made")
    s_v = sem("attention_v_made")
    s_qkc = sem("attention_qk_kept")
    s_vc = sem("attention_v_kept")
    s_qT = sem("attention_q_turned")
    s_kT = sem("attention_k_turned")
    s_kTc = sem("attention_kT_kept")
    s_qbd = sem("attention_q_spread")
    s_sc = sem("attention_scores")
    s_shift = sem("attention_shifted")
    s_exp = sem("attention_exp")
    s_pT = sem("attention_probs_turned")
    s_pTa = sem("attention_probT_kept_act")
    s_pTd = sem("attention_probT_kept_dve")
    s_o = sem("attention_heads_made")
    s_on = sem("attention_heads_scaled")
    s_oT = sem("attention_heads_turned")
    s_oTc = sem("attention_headsT_kept")
    s_y = sem("attention_out_made")
    s_x = sem("attention_x_updated")
    s_one = sem("attention_ones_set")
    s_dve = sem("attention_dve_step")
    steps_ahead = 2 + SLOTS * {"context": 0, "bias": 0, "rope": 1}[kind]
    dve_steps = 2 + SLOTS * {"context": 3, "bias": 4, "rope": 4}[kind]

    def is_first(r):
        return isinstance(r, int) and r == 0

    with nc.Block() as block:

        @block.gpsimd
        def _(pool):
            for g in G:
                pool.memset(vbd[g][:, :, :, :], 0.0).then_inc(s_one, 1)
            pool.wait_ge(s_one, 3 * SLOTS * nth + SLOTS)
            for g in G:
                pool.memset(vbd[g][0:S, :, :, 2 * DH:2 * DH + 1], 1.0).then_inc(s_one, 1)
                pool.memset(vbd[g][S:P, :, :, 2 * DH + 1:VW], 1.0).then_inc(s_one, 1)
            pool.wait_ge(s_one, 3 * SLOTS * (nth + 1))
            with pool.Fori(0, ROUNDS) as r:
                for g in G:
                    if kind == "context":
                        pool.wait_ge(s_qk, LEAD + r * SLOTS)
                        pool.wait_ge(s_v, LEAD + r * SLOTS)
                        pool.tensor_copy(ctxT[g][:, :], w["ctx"][:, bass.ds((r * SLOTS + g) * P, P)])\
                            .then_inc(s_ctx, 1)
                for g in G:
                    pool.wait_ge(s_var, r * SLOTS + before + g + 1)
                    pool.tensor_tensor(rstd[g][:, :], mv[g][:, 1:2], const["minus_half"][:, 0:1], ALU.pow)\
                        .then_inc(s_rstd, 1)

        @block.tensor
        def _(pe):
            if nth == 0:
                pe.sem_inc(s_qk, LEAD)
                pe.sem_inc(s_v, LEAD)

            def turn_x(r, g):
                pe.wait_ge(s_xn, r * SLOTS + before + g + 1)
                for c in range(DC):
                    last = pe.transpose(front[g][:, c * P:(c + 1) * P], xn[g][:, c * P:(c + 1) * P], ident[:, :])
                last.then_inc(s_xT, 1)

            def project(r, g):
                pe.wait_ge(s_xTc, r * SLOTS + before + g + 1)
                if kind == "context":
                    pe.wait_ge(s_ctx, r * SLOTS + before + g + 1)
                    for c in range(DC):
                        pe.matmul(front[g][:, 0:D], xnT[g][:, c, :], w["q"][:, c, :],
                                  start=(c == 0), stop=(c == DC - 1))
                    last = pe.matmul(front[g][:, D:2 * D], ctxT[g][:, :], w["k"][:, :], start=True, stop=True)
                else:
                    for c in range(DC):
                        last = pe.matmul(front[g][:, :], xnT[g][:, c, :], w["qk"][:, c, :],
                                         start=(c == 0), stop=(c == DC - 1))
                last.then_inc(s_qk, 1)
                for b in range(2):
                    for half in range(2):
                        o = vps[g][S * half:S * half + S, b, :]
                        if kind == "context":
                            last = pe.matmul(o, ctxT[g][:, b * S:(b + 1) * S], w["v"][:, :], start=True, stop=True)
                        else:
                            for c in range(DC):
                                last = pe.matmul(o, xnT[g][:, c, b * S:(b + 1) * S], w["v"][:, c, :],
                                                 start=(c == 0), stop=(c == DC - 1))
                last.then_inc(s_v, 1)

            def turn_qk(r, g):
                pe.wait_ge(s_qkc, r * SLOTS + before + g + 1)
                for c in range(DC):
                    last = pe.transpose(front[g][:, c * P:(c + 1) * P], qk[g][:, c * P:(c + 1) * P], ident[:, :])
                last.then_inc(s_qT, 1)
                pe.wait_ge(s_vc, r * SLOTS + before + g + 1)
                for c in range(DC):
                    last = pe.transpose(vps[g][:, 0, c * P:(c + 1) * P],
                                        qk[g][:, D + c * P:D + (c + 1) * P], ident[:, :])
                last.then_inc(s_kT, 1)

            def scores(r, g):
                pe.wait_ge(s_kTc, r * SLOTS + before + g + 1)
                pe.wait_ge(s_qbd, r * SLOTS + before + g + 1)
                pe.wait_ge(s_x, LEAD + r * SLOTS + before)
                for b in range(2):
                    for h in range(H):
                        c, i = divmod(h, H // 2)
                        last = pe.matmul(score[g][S * b:S * b + S, c, i * S:(i + 1) * S],
                                         qbd[g][:, c, i, b * S:(b + 1) * S], kT[g][:, c, b * S:(b + 1) * S],
                                         start=True, stop=True)
                last.then_inc(s_sc, 1)

            def turn_probs(r, g):
                pe.wait_ge(s_exp, r * SLOTS + before + g + 1)
                for j in range(NP):
                    last = pe.transpose(score[g][:, j // 4, (j % 4) * P:(j % 4 + 1) * P],
                                        prob[g][:, 2 * j:2 * j + 2, :], ident[:, :])
                last.then_inc(s_pT, 1)

            def values(r, g):
                pe.wait_ge(s_pTa, r * SLOTS + before + g + 1)
                pe.wait_ge(s_pTd, r * SLOTS + before + g + 1)
                for b in range(2):
                    for j in range(NP):
                        last = pe.matmul(score[g][S * b:S * b + S, 0, j * VW:(j + 1) * VW],
                                         probT[g][:, j, b * S:(b + 1) * S], vbd[g][:, b, j, :],
                                         start=True, stop=True)
                last.then_inc(s_o, 1)

            def turn_heads(r, g):
                pe.wait_ge(s_on, r * SLOTS + before + g + 1)
                for c in range(DC):
                    last = pe.transpose(score[g][:, 1, c * P:(c + 1) * P], heads[g][:, c * P:(c + 1) * P], ident[:, :])
                last.then_inc(s_oT, 1)

            def out(r, g):
                pe.wait_ge(s_oTc, r * SLOTS + before + g + 1)
                for c in range(DC):
                    last = pe.matmul(score[g][:, 0, 0:D], headsT[g][:, c, :], w["o"][:, c, :],
                                     start=(c == 0), stop=(c == DC - 1))
                last.then_inc(s_y, 1)

            pe.wait_ge(s_one, 3 * SLOTS * (nth + 1))
            rounds(pe, (turn_x, project, turn_qk),
                   ((scores, 0), (turn_x, 1), (turn_probs, 0), (project, 1), (values, 0), (turn_heads, 0),
                    (turn_qk, 1), (out, 0)))

        @block.scalar
        def _(act):
            def keep_xT(r, g):
                act.wait_ge(s_xT, r * SLOTS + before + g + 1)
                act.copy(xnT[g][:, :, :], front[g][:, 0:D]).then_inc(s_xTc, 1)

            def keep_qk(r, g):
                if kind == "context":
                    act.wait_ge(s_qk, LEAD + r * SLOTS + before + g + 1)
                    act.copy(qk[g][:, :], front[g][:, :]).then_inc(s_qkc, 1)

            def keep_v(r, g):
                if kind != "bias":
                    act.wait_ge(s_v, LEAD + r * SLOTS + before + g + 1)
                    if is_first(r):
                        act.wait_ge(s_one, 3 * SLOTS * (nth + 1))
                    else:
                        act.wait_ge(s_o, (r - 1) * SLOTS + before + g + 1)
                    v = vps[g][:, :, :].rearrange("p b (j e d) -> p b j e d", e=2, d=DH)
                    act.copy(vbd[g][0:S, :, :, 0:DH], v[0:S, :, :, 0, :])
                    act.copy(vbd[g][S:P, :, :, DH:2 * DH], v[S:P, :, :, 1, :]).then_inc(s_vc, 1)

            def keep_kT(r, g):
                act.wait_ge(s_kT, r * SLOTS + before + g + 1)
                act.copy(kT[g][:, :, :], vps[g][:, 0, :]).then_inc(s_kTc, 1)

            def exps(r, g):
                act.wait_ge(s_shift, r * SLOTS + before + g + 1)
                act.activation(prob[g][:, :, :], prob[g][:, :, :], ACT.Exp, scale=DH ** -0.5).then_inc(s_exp, 1)

            def keep_probT(r, g):
                act.wait_ge(s_pT, r * SLOTS + before + g + 1)
                act.copy(probT[g][:, 0:4, :], score[g][:, 0, :]).then_inc(s_pTa, 1)

            def keep_headsT(r, g):
                act.wait_ge(s_oT, r * SLOTS + before + g + 1)
                act.copy(headsT[g][:, :, :], score[g][:, 1, 0:D]).then_inc(s_oTc, 1)

            rounds(act, (keep_xT, keep_qk, keep_v, keep_kT),
                   ((keep_xT, 1), (exps, 0), (keep_probT, 0), (keep_qk, 1), (keep_v, 1), (keep_headsT, 0),
                    (keep_kT, 1)))

        @block.vector
        def _(dve):
            step = Steps(dve, s_dve)
            if nth == 0:
                dve.sem_inc(s_x, LEAD)

            def normalise(r, slot):
                if slot:
                    return
                x = [x_all[:, bass.ds(r * SLOTS + g, 1), :] for g in G]
                step.each(lambda g: dve.bn_stats(stats[g][:, :], x[g]))
                dve.memset(mv[0][:, 2:3], 0.0)
                step.each(lambda g: dve.bn_aggr(mv[g][:, 0:2], stats[g][:, :]))
                for g in G:
                    dve.tensor_scalar(mv[g][:, 1:2], mv[g][:, 1:2], EPS, None, ALU.add).then_inc(s_var, 1)
                for g in G:
                    dve.wait_ge(s_rstd, r * SLOTS + before + g + 1)
                    dve.tensor_scalar(xn[g][:, :], x[g], mv[g][:, 0:1], rstd[g][:, 0:1], ALU.subtract, ALU.mult)\
                        .then_inc(s_xn, 1)

            def keep_v(r, g):
                if kind == "bias":
                    dve.wait_ge(s_v, LEAD + r * SLOTS + before + g + 1)
                    if is_first(r):
                        dve.wait_ge(s_one, 3 * SLOTS * (nth + 1))
                    else:
                        dve.wait_ge(s_o, (r - 1) * SLOTS + before + g + 1)
                    for e in range(2):
                        rows = slice(S * e, S * e + S)
                        for b in range(2):
                            v = vps[g][rows, b, :].rearrange("p (j e d) -> p j e d", e=2, d=DH)[:, :, e, :]
                            bv = w["bv"][rows, :].rearrange("p (j e d) -> p j e d", e=2, d=DH)[:, :, e, :]
                            last = dve.tensor_tensor(vbd[g][rows, b, :, e * DH:(e + 1) * DH], v, bv, ALU.add)
                    last.then_inc(s_vc, 1)

            def keep_qk(r, g):
                if kind == "context":
                    return
                dve.wait_ge(s_qk, LEAD + r * SLOTS + before + g + 1)
                if kind == "bias":
                    dve.tensor_tensor(qk[g][:, :], front[g][:, :], w["bqk"][:, :], ALU.add).then_inc(s_qkc, 1)
                else:
                    t2p = t2[g][:, :].rearrange("p (n e) -> p n e", e=2)
                    fp = front[g][:, :].rearrange("p (n e) -> p n e", e=2)
                    sn = w["sin"][:, :].rearrange("p (n e) -> p n e", e=2)
                    dve.tensor_tensor(t1[g][:, :], front[g][:, :], w["cos"][:, :], ALU.mult)
                    dve.tensor_tensor(t2p[:, :, 0], fp[:, :, 1], sn[:, :, 0], ALU.mult)
                    step.done(dve.tensor_tensor(t2p[:, :, 1], fp[:, :, 0], sn[:, :, 1], ALU.mult))
                    dve.tensor_tensor(qk[g][:, :], t1[g][:, :], t2[g][:, :], ALU.add).then_inc(s_qkc, 1)

            def spread_q(r, g):
                dve.wait_ge(s_qT, r * SLOTS + before + g + 1)
                for c in range(DC):
                    q = front[g][:, c * P:(c + 1) * P].unsqueeze(1).broadcast_to([P, H // 2, P])
                    m = head_rows[:, :].unsqueeze(2).broadcast_to([P, H // 2, P])
                    last = dve.tensor_tensor(qbd[g][:, c, :, :], q, m, ALU.mult)
                last.then_inc(s_qbd, 1)

            def shift(r, g):
                dve.wait_ge(s_sc, r * SLOTS + before + g + 1)
                sc = score[g][:, :, :].rearrange("p c (i k) -> p (c i) k", k=S)
                step.done(dve.tensor_tensor(prob[g][:, :, :], sc, mask[:, :].unsqueeze(1).broadcast_to([P, H, S]), ALU.add))
                step.done(dve.tensor_reduce(rmax[g][:, :], prob[g][:, :, :], AX.X, ALU.max))
                dve.tensor_tensor(prob[g][:, :, :], prob[g][:, :, :],
                                  rmax[g][:, :].unsqueeze(2).broadcast_to([P, H, S]), ALU.subtract)\
                    .then_inc(s_shift, 1)

            def keep_probT(r, g):
                dve.wait_ge(s_pT, r * SLOTS + before + g + 1)
                dve.tensor_copy(probT[g][:, 4:8, :], score[g][:, 1, :]).then_inc(s_pTd, 1)

            def scale_heads(r, g):
                dve.wait_ge(s_o, r * SLOTS + before + g + 1)
                o = score[g][:, 0, 0:NP * VW].rearrange("p (j v) -> p j v", v=VW)
                rd = rden[g][:, :].rearrange("p (j e) -> p j e", e=2)
                step.done(dve.reciprocal(rd, o[:, :, 2 * DH:VW]))
                dve.tensor_tensor(heads[g][:, :].rearrange("p (j e d) -> p j e d", e=2, d=DH),
                                  o[:, :, 0:2 * DH].rearrange("p j (e d) -> p j e d", d=DH),
                                  rd.unsqueeze(3).broadcast_to([P, NP, 2, DH]), ALU.mult).then_inc(s_on, 1)

            def update_x(r, g):
                dve.wait_ge(s_y, r * SLOTS + before + g + 1)
                x = x_all[:, bass.ds(r * SLOTS + g, 1), :]
                ins = dve.tensor_tensor(x, score[g][:, 0, 0:D].unsqueeze(1), x, ALU.add)
                if kind == "bias":
                    step.done(ins)
                    ins = dve.tensor_tensor(x, x, w["bo"][:, :].unsqueeze(1), ALU.add)
                ins.then_inc(s_x, 1)

            def start(r):
                step.start(r * dve_steps + steps_before + steps_ahead)

            step.start(steps_before)

            rounds(dve, (normalise, keep_qk, keep_v, spread_q),
                   ((normalise, 1), (shift, 0), (keep_probT, 0), (keep_qk, 1), (keep_v, 1), (scale_heads, 0),
                    (spread_q, 1), (update_x, 0)), start)
    return steps_before + ROUNDS * dve_steps


CH, CK, CQ = 16, 128, 192
HALF = CQ // 2
CP = CH // 2
QW = CP * S
SKP = 1608
KQ = SKP // 4
KC = 402
NKC = SKP // KC
NKT = -(-SK // P)
NSUM = NKT - 1
PIECES = 16


def context_weights(sb, prep_sb, a):
    kept = (sb("cx_wbig", [P, DC, CP, 2 * CQ]), sb("cx_mw", [P, CP, 2, 3, DCX]), sb("cx_wvo", [P, CP, D]))
    shapes = {"wq": [P, CH, D], "wkcq": [P, CH, CQ], "wqrT": [DCX, CH, 2, CQ], "wkrT": [DCX, CH, DCX],
              "wkckv": [P, CH, DCX], "woT": [P, CH, D]}
    raw = {key: prep_sb(f"cx_{key}", shape) for key, shape in shapes.items()}
    return kept, raw, [(raw[key][tuple(slice(None) for _ in shape)], a[f"cx_{key}"])
                       for key, shape in shapes.items()]


def absorb_weights(nc, sem, raw, wbig, mw, wvo):
    wq, wkcq, wqrT, wkrT, wkckv, woT = (raw[key] for key in ("wq", "wkcq", "wqrT", "wkrT", "wkckv", "woT"))
    with ExitStack() as prep:
        bank = [prep.enter_context(nc.psum_tensor(f"cx_prep{i}", [P, 512], F32)) for i in range(8)]
        s_made = sem("cx_prep_made")
        s_dve = sem("cx_prep_kept_dve")
        s_act = sem("cx_prep_kept_act")

        def big(pe, o, n):
            j, c = divmod(n, DC)
            for e in range(2):
                last = pe.matmul(o[:, e * CQ:(e + 1) * CQ], wq[:, 2 * j + e, c * P:(c + 1) * P],
                                 wkcq[:, 2 * j + e, :], start=True, stop=True)
            return last

        def rotated(pe, o, j):
            for cs in range(2):
                for e, tile, rows, cols in ((0, 0, slice(0, P), slice(0, P)), (0, 1, slice(0, 64), slice(P, CQ)),
                                            (1, 1, slice(64, P), slice(P, CQ)), (1, 2, slice(0, P), slice(0, P))):
                    at = (cs * 3 + tile) * DCX
                    last = pe.matmul(o[rows, at:at + DCX], wqrT[:, 2 * j + e, cs, cols], wkrT[:, 2 * j + e, :],
                                     start=True, stop=True)
            return last

        def values(pe, o, j):
            for e in range(2):
                last = pe.matmul(o[DCX * e:DCX * e + DCX, 0:D], wkckv[:, 2 * j + e, :], woT[:, 2 * j + e, :],
                                 start=True, stop=True)
            return last

        jobs = [(big, n, wbig[:, n % DC, n // DC, :], 2 * CQ) for n in range(CP * DC)]
        jobs += [(rotated, j, mw[:, j, :, :, :], 6 * DCX) for j in range(CP)]
        jobs += [(values, j, wvo[:, j, :], D) for j in range(CP)]
        with nc.Block() as block:

            @block.tensor
            def _(pe):
                for n, (product, j, _, _) in enumerate(jobs):
                    if n >= 8:
                        pe.wait_ge(s_act if n % 2 else s_dve, (n - 8) // 2 + 1)
                    product(pe, bank[n % 8], j).then_inc(s_made, 1)

            @block.vector
            def _(dve):
                for n, (_, _, kept, w) in enumerate(jobs):
                    if n % 2 == 0:
                        dve.wait_ge(s_made, n + 1)
                        dve.tensor_copy(kept, bank[n % 8][:, 0:w]).then_inc(s_dve, 1)

            @block.scalar
            def _(act):
                for n, (_, _, kept, w) in enumerate(jobs):
                    if n % 2 == 1:
                        act.wait_ge(s_made, n + 1)
                        act.copy(kept, bank[n % 8][:, 0:w]).then_inc(s_act, 1)


def context_attention(nc, sb, pb, sem, a, x_all, const, wbig, mw, wvo):
    ident = const["ident"]
    tab = sb("cx_tab", [P, 2, 3, S])
    kcos = sb("cx_kcos", [DCX, SKP])
    ksin = sb("cx_ksin", [DCX, SKP])
    ctx = sb("cx_ctx", [DCX, SKP])
    ctxr = sb("cx_ctxr", [DCX, SKP])
    kr = sb("cx_kr", [DCX, SKP])
    k1 = [sb(f"cx_k1{i}", [P, SKP], F32R) for i in range(2)]
    k2 = [sb(f"cx_k2{i}", [P, SKP], F32R) for i in range(2)]
    kv = [sb(f"cx_kv{i}", [P, NKT, DCX]) for i in range(2)]
    q1 = [sb(f"cx_q1{i}", [P, 2, CP, S], F32R) for i in range(2)]
    q2 = [sb(f"cx_q2{i}", [P, 2, CP, S], F32R) for i in range(2)]
    qs = sb("cx_qs", [DCX, 2, CP, S])
    stats = sb("cx_stats", [P, 6])
    mv = sb("cx_mv", [P, 3])
    rstd = sb("cx_rstd", [P, 1])
    xn = sb("cx_xn", [P, D])
    xnT = sb("cx_xnT", [P, DC, P])
    turn = [sb(f"cx_turn{i}", [P, 2, 3, 2, S]) for i in range(2)]
    RING = 3
    prob = [sb(f"cx_prob{i}", [P, 2, QW]) for i in range(RING + 1)]
    acc = [sb(f"cx_acc{e}", [P, QW]) for e in range(2)]
    ones = sb("cx_ones", [P, DCX])
    identb = sb("cx_identb", [P, P], BF16)
    mhalf = sb("cx_mhalf", [P, PIECES // 2, 2])
    nmax = sb("cx_nmax", [P, PIECES // 2])
    nmh = sb("cx_nmh", [P, PIECES // 2], BF16)
    nml = sb("cx_nml", [P, PIECES // 2], BF16)
    rden = sb("cx_rden", [P, QW])
    summed = sb("cx_summed", [P, CP, S])
    heads = sb("cx_heads", [P, CP, 2, S])

    mx = [pb(f"cx_mx{i}", [P, 2, 512]) for i in range(2)]
    st = [pb(f"cx_st{e}", [P, 512]) for e in range(2)]
    av = pb("cx_av", [P, 512])
    misc = pb("cx_misc", [P, 512])

    load(nc, sem("cx_loaded"), [(tab[:, :, :, :], a["cx_tab"]), (kcos[:, :], a["cx_kcos"]),
                                (ksin[:, :], a["cx_ksin"])])

    s_set = sem("cx_padding_set")
    s_one = sem("cx_ones_set")
    s_ctx = sem("cx_context_loaded")
    s_rope = sem("cx_context_turned")
    s_kr = sem("cx_keys_summed")
    s_k1 = sem("cx_kh_kept")
    s_k2 = sem("cx_k2_kept")
    s_kl = sem("cx_kl_kept")
    s_kt = sem("cx_keys_transposed")
    s_kv = sem("cx_kv_kept")
    s_var = sem("cx_variance")
    s_rstd = sem("cx_rstd_made")
    s_xn = sem("cx_normalised")
    s_xT = sem("cx_x_turned")
    s_xTc = sem("cx_xT_kept")
    s_big = sem("cx_big_queries")
    s_rot = sem("cx_queries_rotated")
    s_eff = sem("cx_queries_made")
    s_q1a = sem("cx_even_q1_kept")
    s_q2a = sem("cx_even_q2_kept")
    s_q1b = sem("cx_odd_q1_kept")
    s_q2b = sem("cx_odd_q2_kept")
    s_mx = sem("cx_max_scores")
    s_mr = sem("cx_max_reduced")
    s_nm = sem("cx_negated_max")
    s_row = sem("cx_max_row")
    s_rowk = sem("cx_max_row_kept")
    s_st = sem("cx_scores")
    s_exp = sem("cx_exp")
    s_av = sem("cx_values_added")
    s_acc = [sem("cx_even_sum"), sem("cx_odd_sum")]
    s_sum = sem("cx_denominators")
    s_rcp = sem("cx_reciprocals")
    s_avk = sem("cx_summed_kept")
    s_hd = sem("cx_heads_scaled")
    s_out = sem("cx_out")
    s_x = sem("cx_x_updated")
    s_dve = sem("cx_dve_step")

    def nk(kt):
        return min(P, SK - kt * P)

    HEADS_AT = 2
    OUT_AT = 4
    TURN_AT = 6
    ROWS_AT = NKT - 3
    SUM_AT = (8, 9, 11, 12)

    def pieces(e, kt, third):
        start, end = 3 * (5 if e else 3), 3 * ROWS_AT
        first = lambda k: min(max(0, -(-(k - start) * PIECES // (end - start))), PIECES)
        return range(first(3 * kt + third), first(3 * kt + third + 1))

    def slot(kt):
        return kt % RING if kt < NKT - 1 else RING

    def batches(engine, before, batch):
        before()
        batch(0, 0, 0, True, True)
        with engine.Fori(0, NT - 2) as t:
            batch(2 * t + 1, t, 1, True, True)
            batch(2 * t + 2, t + 1, 0, True, True)
        batch(B - 3, NT - 2, 1, True, True)
        batch(B - 2, NT - 1, 0, False, True)
        batch(B - 1, NT - 1, 1, False, False)

    def is_first(n):
        return isinstance(n, int) and n == 0

    with nc.Block() as block:

        @block.sync
        def _(sp):
            def fetch(n):
                sp.dma_start(ctx[:, :], a["cx_ctxT"][bass.ds(n, 1), :, :]).then_inc(s_ctx, 16)
                sp.dma_start(ctxr[:, :], a["cx_ctxrT"][bass.ds(n, 1), :, :]).then_inc(s_ctx, 16)

            fetch(0)
            with sp.Fori(1, B) as n:
                sp.wait_ge(s_kr, n * NKC)
                fetch(n)

        @block.gpsimd
        def _(pool):
            def rotate(n, c):
                cols = slice(c * KC, (c + 1) * KC)
                if c == 0:
                    pool.wait_ge(s_ctx, 32 * n + 32)
                pool.tensor_tensor(ctx[:, cols], ctx[:, cols], kcos[:, cols], ALU.mult)
                pool.tensor_tensor(ctxr[:, cols], ctxr[:, cols], ksin[:, cols], ALU.mult).then_inc(s_rope, 1)

            def root(t):
                pool.wait_ge(s_var, t + 1)
                pool.tensor_tensor(rstd[:, :], mv[:, 1:2], const["minus_half"][:, 0:1], ALU.pow).then_inc(s_rstd, 1)

            def add(n, kt):
                rows = slice(0, nk(kt))
                pool.wait_ge(s_exp, n * 2 * NKT + 2 * kt + 1)
                if kt == 1:
                    pool.wait_ge(s_sum, n)
                else:
                    pool.wait_ge(s_acc[0], n * NSUM + kt - 1)
                sofar = prob[0][rows, 0, :] if kt == 1 else acc[0][rows, :]
                pool.tensor_tensor(acc[0][rows, :], sofar, prob[slot(kt)][rows, 0, :], ALU.add)\
                    .then_inc(s_acc[0], 1)

            def before():
                for i in range(2):
                    pool.memset(k2[i][DCX:P, :].bitcast(F32), 0.0).then_inc(s_set, 1)
                    pool.memset(q2[i][DCX:P, :, :, :].bitcast(F32), 0.0).then_inc(s_set, 1)
                pool.wait_ge(s_set, 4)
                for i in range(2):
                    pool.memset(k2[i][DCX:DCX + 1, :].bitcast(F32), 1.0).then_inc(s_set, 1)
                pool.wait_ge(s_set, 6)
                root(0)
                for n in range(2):
                    for c in range(NKC):
                        rotate(n, c)

            def batch(n, t, e, more, next):
                for kt in range(1, NKT):
                    add(n, kt)
                    if more and kt % 2 == 1 and 3 <= kt < 3 + 2 * NKC:
                        rotate(n + 2, kt // 2 - 1)
                    if more and e == 0 and kt == ROWS_AT:
                        root(t + 1)

            batches(pool, before, batch)

        @block.tensor
        def _(pe):
            def turn_keys(n, q):
                pe.wait_ge(s_kr, (n + 1) * NKC)
                if q == 1:
                    pe.wait_ge(s_kv, 2 * n + 1)
                for kt in range(8 * q, min(8 * q + 8, NKT)):
                    o, keys = misc[0:nk(kt), (kt % 8) * DCX:(kt % 8 + 1) * DCX], kr[:, kt * P:kt * P + nk(kt)]
                    if kt == 8 * q:
                        pe.matmul(o, keys, ident[0:DCX, 0:DCX], start=True, stop=True)
                    else:
                        last = pe.transpose(o, keys, ident[0:DCX, 0:DCX])
                last.then_inc(s_kt, 1)

            def turn_x(t):
                pe.wait_ge(s_xn, t + 1)
                if not is_first(t):
                    pe.wait_ge(s_mr, 2 * t * PIECES)
                for c in range(DC):
                    last = pe.transpose(mx[0][:, 0, c * P:(c + 1) * P], xn[:, c * P:(c + 1) * P], ident[:, :])
                last.then_inc(s_xT, 1)

            def big(t, j):
                if j == 0:
                    pe.wait_ge(s_xTc, t + 1)
                if j >= 2:
                    pe.wait_ge(s_rot, t * CP + j - 1)
                for tile in range(3):
                    for c in range(DC):
                        last = pe.matmul(mx[j % 2][:, 0, tile * P:(tile + 1) * P],
                                         wbig[:, c, j, tile * P:(tile + 1) * P], xnT[:, c, :],
                                         start=(c == 0), stop=(c == DC - 1))
                last.then_inc(s_big, 1)

            def effective(t, j):
                pe.wait_ge(s_rot, t * CP + j + 1)
                at = (j % 4) * P
                for cs in range(2):
                    for i in range(2):
                        for e in range(2):
                            tile = (0, 2)[e] if i == 0 else 1
                            rows = slice(0, P) if i == 0 else slice(64 * e, 64 * e + 64)
                            last = pe.matmul(mx[j // 4][DCX * e:DCX * e + DCX, 1, at:at + P],
                                             mw[rows, j, cs, tile, :], turn[j % 2][rows, cs, tile, :, :],
                                             start=(cs == 0 and i == 0), stop=(cs == 1 and i == 1))
                last.then_inc(s_eff, 1)

            def queries(t, j):
                if 2 <= j < CP + 2:
                    effective(t, j - 2)
                if j < CP:
                    big(t, j)

            def max_scores(t, n, e, i):
                b = i % 2
                if i == 0:
                    pe.wait_ge(s_kl, n + 1)
                    pe.wait_ge(s_k2, n + 1)
                    if e == 0:
                        pe.wait_ge(s_q1a, 2 * t + 2)
                        pe.wait_ge(s_q2a, 2 * t + 2)
                    else:
                        pe.wait_ge(s_q1b, t + 1)
                        pe.wait_ge(s_q2b, t + 1)
                if not (is_first(n) and i < 2):
                    pe.wait_ge(s_mr, n * PIECES + max(i - 1, 0))
                q = q1[e][:, :, :, :].rearrange("p e j s -> p (e j s)")[:, (i // 2) * P:(i // 2 + 1) * P]
                for h in range(2):
                    lo = (2 * b + h) * KQ
                    last = pe.matmul(mx[b][:, h, 0:KQ], q, k1[e][:, lo:lo + KQ], start=True, stop=True)
                last.then_inc(s_mx, 1)

            def max_rows(n, p):
                if p == 0:
                    pe.wait_ge(s_nm, n + 1)
                    pe.wait_ge(s_kv, 2 * n + 2)
                else:
                    pe.wait_ge(s_rowk, 2 * n + 1)
                for i in range(4):
                    for part, (w, lo) in enumerate(((nmh, True), (nml, False))):
                        last = pe.matmul(misc[0:1, i * P:(i + 1) * P], w[:, 4 * p + i:4 * p + i + 1], identb[:, :],
                                         start=(part == 0), stop=(part == 1))
                last.then_inc(s_row, 1)

            def scores(n, e, kt, p):
                keys = slice(kt * P, kt * P + nk(kt))
                g = 2 * kt + p
                if not (is_first(n) and g < 2):
                    pe.wait_ge(s_exp, n * 2 * NKT + g - 1)
                if g == 0:
                    pe.wait_ge(s_rowk, 2 * n + 2)
                pe.matmul(st[p][0:nk(kt), :], k1[e][:, keys], q1[e][:, p, :, :], start=True, stop=False)
                pe.matmul(st[p][0:nk(kt), :], k2[e][:, keys], q2[e][:, p, :, :], start=False, stop=True)\
                    .then_inc(s_st, 1)

            def values(n, e, kt):
                pe.wait_ge(s_exp, n * 2 * NKT + 2 * kt + 2)
                if kt == 0:
                    pe.wait_ge(s_kv, 2 * n + 2)
                    if not is_first(n):
                        pe.wait_ge(s_avk, n)
                for p in range(2):
                    last = pe.matmul(av[DCX * p:DCX * p + DCX, :], kv[e][0:nk(kt), kt, :],
                                     prob[slot(kt)][0:nk(kt), p, :], start=(kt == 0), stop=(kt == NKT - 1))
                last.then_inc(s_av, 1)

            def denominators(n):
                for p in range(2):
                    pe.wait_ge(s_acc[p], (n + 1) * NSUM)
                pe.wait_ge(s_rowk, min(2 * n + 4, 2 * B) if isinstance(n, int) else 2 * n + 4)
                for p in range(2):
                    last = pe.matmul(misc[DCX * p:DCX * p + DCX, :], ones[:, :], acc[p][:, :], start=True, stop=True)
                last.then_inc(s_sum, 1)

            def out(t):
                pe.wait_ge(s_hd, 2 * t + 2)
                for j in range(CP):
                    last = pe.matmul(misc[:, 0:D], heads[:, j, :, :], wvo[:, j, :],
                                     start=(j == 0), stop=(j == CP - 1))
                last.then_inc(s_out, 1)

            def before():
                pe.wait_ge(s_set, 6)
                pe.wait_ge(s_one, 1)
                turn_keys(0, 0)
                turn_keys(0, 1)
                turn_x(0)
                for j in range(CP + 2):
                    queries(0, j)
                for i in range(PIECES):
                    max_scores(0, 0, 0, i)
                max_rows(0, 0)
                max_rows(0, 1)
                scores(0, 0, 0, 0)
                scores(0, 0, 0, 1)

            def batch(n, t, e, more, next):
                for kt in range(NKT):
                    if kt == 0 and more and e == 1:
                        turn_x(t + 1)
                    for third in range(3):
                        if third == 2:
                            values(n, e, kt)
                        elif kt + 1 < NKT:
                            scores(n, e, kt + 1, third)
                        elif next:
                            scores(n + 1, 1 - e, 0, third)
                        if more and e == 1 and third < 2 and kt <= CP // 2:
                            queries(t + 1, 2 * kt + third)
                        if next:
                            for i in pieces(e, kt, third):
                                max_scores(t + e, n + 1, 1 - e, i)
                    if kt == 0 and not is_first(n):
                        denominators(n - 1)
                    if kt == OUT_AT and e == 0 and not is_first(n):
                        out(t - 1)
                    if kt in (TURN_AT, TURN_AT + 1) and next:
                        if kt == TURN_AT and not is_first(n):
                            if e == 0:
                                pe.wait_ge(s_x, t)
                            else:
                                pe.wait_ge(s_hd, n)
                        turn_keys(n + 1, kt - TURN_AT)
                    if kt in (ROWS_AT, ROWS_AT + 1) and next:
                        max_rows(n + 1, kt - ROWS_AT)

            batches(pe, before, batch)
            denominators(B - 1)
            out(NT - 1)

        @block.scalar
        def _(act):
            def keep_keys(n, e, k, s_k):
                act.wait_ge(s_kr, (n + 1) * NKC)
                if not isinstance(n, int) or n >= 2:
                    act.wait_ge(s_st, (n - 1) * 2 * NKT)
                act.copy(k[e][0:DCX, :], kr[:, :]).then_inc(s_k, 1)

            def keep_kv(n, e, q):
                act.wait_ge(s_kt, 2 * n + q + 1)
                if q == 0:
                    if not isinstance(n, int) or n >= 2:
                        act.wait_ge(s_av, (n - 1) * NKT)
                    act.copy(kv[e][:, 0:8, :], misc[:, :]).then_inc(s_kv, 1)
                else:
                    m = nk(NKT - 1)
                    act.copy(kv[e][:, 8:NKT - 1, :], misc[:, 0:(NKT - 9) * DCX])
                    act.copy(kv[e][0:m, NKT - 1, :], misc[0:m, (NKT - 9) * DCX:(NKT - 8) * DCX]).then_inc(s_kv, 1)

            def keep_x(t):
                act.wait_ge(s_xT, t + 1)
                act.copy(xnT[:, :, :], mx[0][:, 0, 0:D]).then_inc(s_xTc, 1)

            def keep_queries(t, g):
                act.wait_ge(s_eff, t * CP + 4 * g + 4)
                if g == 0 and not is_first(t):
                    act.wait_ge(s_st, (2 * t - 1) * 2 * NKT)
                    act.wait_ge(s_q2b, t)
                for e in range(2):
                    q = mx[g][DCX * e:DCX * e + DCX, 1, :].rearrange("p (j b s) -> p j b s", b=2, s=S)
                    for up in range(2):
                        act.copy(q1[0][DCX * up:DCX * up + DCX, e, 4 * g:4 * g + 4, :], q[:, :, 0, :])
                    last = act.copy(qs[:, e, 4 * g:4 * g + 4, :], q[:, :, 1, :])
                last.then_inc(s_q1a, 1)

            def odd_queries(t):
                if not is_first(t):
                    act.wait_ge(s_st, 2 * t * 2 * NKT)
                for up in range(2):
                    last = act.copy(q1[1][DCX * up:DCX * up + DCX, :, :, :], qs[:, :, :, :])
                last.then_inc(s_q1b, 1)

            def exps(n, kt):
                rows = slice(0, nk(kt))
                for p in range(2):
                    act.wait_ge(s_st, n * 2 * NKT + 2 * kt + p + 1)
                    if p == 0 and not (is_first(n) and (kt < RING or kt == NKT - 1)):
                        if kt == NKT - 1:
                            use, m = n - 1, NKT - 1
                        elif kt < RING:
                            use, m = n - 1, NKT - 1 - RING + kt
                        else:
                            use, m = n, kt - RING
                        act.wait_ge(s_av, use * NKT + m + 1)
                        for s in s_acc:
                            act.wait_ge(s, use * NSUM + max(m, 1))
                    act.activation(prob[slot(kt)][rows, p, :], st[p][rows, :], ACT.Exp).then_inc(s_exp, 1)

            def keep_rows(n, e, p):
                act.wait_ge(s_row, 2 * n + p + 1)
                act.copy(q2[e][DCX:DCX + 1, p, :, :], misc[0:1, :]).then_inc(s_rowk, 1)

            def keep_summed(n):
                act.wait_ge(s_av, (n + 1) * NKT)
                if not is_first(n):
                    act.wait_ge(s_hd, n)
                act.copy(summed[:, :, :], av[:, :]).then_inc(s_avk, 1)

            def before():
                act.wait_ge(s_set, 6)
                keep_keys(0, 0, k1, s_k1)
                keep_keys(0, 0, k2, s_k2)
                keep_kv(0, 0, 0)
                keep_kv(0, 0, 1)
                keep_x(0)
                for g in range(2):
                    keep_queries(0, g)
                keep_rows(0, 0, 0)
                keep_rows(0, 0, 1)

            def batch(n, t, e, more, next):
                for kt in range(NKT):
                    exps(n, kt)
                    if kt == 0 and not is_first(n):
                        keep_summed(n - 1)
                    if kt == 0 and more and e == 1:
                        keep_x(t + 1)
                    if kt == 0 and e == 0:
                        odd_queries(t)
                    if kt == 0 and next:
                        keep_keys(n + 1, 1 - e, k1, s_k1)
                    if kt == 1 and next:
                        keep_keys(n + 1, 1 - e, k2, s_k2)
                    if kt in (3, 4) and more and e == 1:
                        keep_queries(t + 1, kt - 3)
                    if kt in (TURN_AT + 1, TURN_AT + 2) and next:
                        keep_kv(n + 1, 1 - e, kt - TURN_AT - 1)
                    if kt in (ROWS_AT + 1, ROWS_AT + 2) and next:
                        keep_rows(n + 1, 1 - e, kt - ROWS_AT - 1)

            batches(act, before, batch)
            keep_summed(B - 1)

        @block.vector
        def _(dve):
            step = Steps(dve, s_dve)

            def sum_keys(n, c):
                cols = slice(c * KC, (c + 1) * KC)
                dve.wait_ge(s_rope, n * NKC + c + 1)
                if c == 0 and not is_first(n):
                    dve.wait_ge(s_k2, n)
                    dve.wait_ge(s_kt, 2 * n)
                    dve.wait_ge(s_kl, n)
                dve.tensor_tensor(kr[:, cols], ctx[:, cols], ctxr[:, cols], ALU.add).then_inc(s_kr, 1)

            def keep_kl(n, e):
                dve.wait_ge(s_k1, n + 1)
                dve.wait_ge(s_kr, (n + 1) * NKC)
                dve.tensor_tensor(k1[e][DCX:P, :], kr[:, :], k1[e][0:DCX, :].bitcast(F32), ALU.subtract)\
                    .then_inc(s_kl, 1)

            def normalise(t, base):
                step.start(base)
                x = x_all[:, bass.ds(t, 1), :]
                step.done(dve.bn_stats(stats[:, :], x))
                dve.memset(mv[:, 2:3], 0.0)
                step.done(dve.bn_aggr(mv[:, 0:2], stats[:, :]))
                dve.tensor_scalar(mv[:, 1:2], mv[:, 1:2], EPS, None, ALU.add).then_inc(s_var, 1)
                dve.wait_ge(s_rstd, t + 1)
                if not is_first(t):
                    dve.wait_ge(s_xT, t)
                dve.tensor_scalar(xn[:, :], x, mv[:, 0:1], rstd[:, 0:1], ALU.subtract, ALU.mult).then_inc(s_xn, 1)

            def rotate(t, j):
                dve.wait_ge(s_big, t * CP + j + 1)
                if j >= 2:
                    dve.wait_ge(s_eff, t * CP + j - 1)
                q = mx[j % 2][:, 0, 0:3 * P].rearrange("p (m b s) -> p m b s", b=2, s=S)
                for cs in range(2):
                    last = dve.tensor_tensor(turn[j % 2][:, cs, :, :, :], q,
                                             tab[:, cs, :, :].unsqueeze(2).broadcast_to([P, 3, 2, S]), ALU.mult)
                last.then_inc(s_rot, 1)

            def split(t, g):
                dve.wait_ge(s_q1a, 2 * t + g + 1)
                for e in range(2):
                    q = mx[g][DCX * e:DCX * e + DCX, 1, :].rearrange("p (j b s) -> p j b s", b=2, s=S)
                    last = dve.tensor_tensor(q2[0][0:DCX, e, 4 * g:4 * g + 4, :], q[:, :, 0, :],
                                             q1[0][0:DCX, e, 4 * g:4 * g + 4, :].bitcast(F32), ALU.subtract)
                last.then_inc(s_q2a, 1)

            def odd_queries(t):
                dve.wait_ge(s_q1b, t + 1)
                dve.tensor_tensor(q2[1][0:DCX, :, :, :], qs[:, :, :, :], q1[1][0:DCX, :, :, :].bitcast(F32),
                                  ALU.subtract).then_inc(s_q2b, 1)

            def reduce_max(n, i):
                dve.wait_ge(s_mx, n * PIECES + i + 1)
                dve.tensor_reduce(mhalf[:, i // 2, i % 2:i % 2 + 1], mx[i % 2][:, :, 0:KQ], AX.XY, ALU.max)\
                    .then_inc(s_mr, 1)

            def negate_max(n, base):
                step.start(base)
                dve.wait_ge(s_mr, (n + 1) * PIECES)
                step.done(dve.tensor_reduce(nmax[:, :], mhalf[:, :, :], AX.X, ALU.max, negate=True))
                step.done(dve.tensor_copy(nmh[:, :], nmax[:, :]))
                dve.tensor_tensor(nml[:, :], nmax[:, :], nmh[:, :], ALU.subtract).then_inc(s_nm, 1)

            def add(n, kt):
                rows = slice(0, nk(kt))
                dve.wait_ge(s_exp, n * 2 * NKT + 2 * kt + 2)
                if kt == 1:
                    dve.wait_ge(s_sum, n)
                else:
                    dve.wait_ge(s_acc[1], n * NSUM + kt - 1)
                sofar = prob[0][rows, 1, :] if kt == 1 else acc[1][rows, :]
                dve.tensor_tensor(acc[1][rows, :], sofar, prob[slot(kt)][rows, 1, :], ALU.add)\
                    .then_inc(s_acc[1], 1)

            def invert(n, half):
                dve.wait_ge(s_sum, n + 1)
                cols = slice(half * QW // 2, (half + 1) * QW // 2)
                dve.reciprocal(rden[:, cols], misc[:, cols]).then_inc(s_rcp, 1)

            def scale_heads(n, e):
                dve.wait_ge(s_rcp, 2 * n + 2)
                dve.wait_ge(s_avk, n + 1)
                dve.tensor_tensor(heads[:, :, e, :], summed[:, :, :], rden[:, :].rearrange("p (j s) -> p j s", s=S),
                                  ALU.mult).then_inc(s_hd, 1)

            def update_x(t):
                dve.wait_ge(s_out, t + 1)
                x = x_all[:, bass.ds(t, 1), :]
                dve.tensor_tensor(x, misc[:, 0:D].unsqueeze(1), x, ALU.add).then_inc(s_x, 1)

            def before():
                dve.memset(ones[:, :], 1.0)
                dve.tensor_copy(identb[:, :], ident[:, :]).then_inc(s_one, 1)
                normalise(0, 0)
                for c in range(NKC):
                    sum_keys(0, c)
                keep_kl(0, 0)
                for j in range(CP):
                    rotate(0, j)
                    if j == 5:
                        split(0, 0)
                split(0, 1)
                for c in range(NKC):
                    sum_keys(1, c)
                for i in range(PIECES):
                    reduce_max(0, i)
                negate_max(0, 2)

            def batch(n, t, e, more, next):
                base = 4 + 6 * t + (4 if e else 0)
                for kt in range(NKT):
                    for third in range(3):
                        if third == 1 and kt:
                            add(n, kt)
                        if third < 2 and more and e == 1 and kt < CP // 2:
                            rotate(t + 1, 2 * kt + third)
                        if next:
                            for i in pieces(e, kt, third):
                                reduce_max(n + 1, i)
                    if kt == 0 and e == 0:
                        odd_queries(t)
                    if kt == 1 and next:
                        keep_kl(n + 1, 1 - e)
                    if kt in (HEADS_AT, HEADS_AT + 1) and not is_first(n):
                        invert(n - 1, kt - HEADS_AT)
                        if kt == HEADS_AT + 1:
                            scale_heads(n - 1, 1 - e)
                    if kt in (3, 4) and more and e == 1:
                        split(t + 1, kt - 3)
                    if kt == OUT_AT + 1 and e == 0 and not is_first(n):
                        update_x(t - 1)
                    if more and kt in SUM_AT:
                        sum_keys(n + 2, SUM_AT.index(kt))
                    if more and e == 0 and kt == ROWS_AT:
                        normalise(t + 1, base + (2 if next else 0))
                    if next and kt == ROWS_AT - 1:
                        negate_max(n + 1, base)

            batches(dve, before, batch)
            invert(B - 1, 0)
            invert(B - 1, 1)
            scale_heads(B - 1, 1)
            update_x(NT - 1)


def context_layout(inp, a, rows, spread):
    f = np.float32
    a["cx_wq"] = inp["L1_xattn_Wq"].reshape(CH, CK, D).transpose(1, 0, 2)
    odd = np.concatenate([np.arange(P, CQ), np.arange(P)])
    wkcq = inp["L1_xattn_w_kc_q"].transpose(1, 0, 2)
    a["cx_wkcq"] = np.stack([wkcq[:, 0::2], wkcq[:, 1::2][:, :, odd]], axis=2).reshape(CK, CH, CQ)
    wqr = inp["L1_xattn_W_qr"]
    a["cx_wqrT"] = np.stack([wqr, np.roll(wqr, HALF, axis=1)], axis=1).transpose(3, 0, 1, 2)
    a["cx_wkrT"] = inp["L1_xattn_W_kr"].transpose(2, 0, 1)
    a["cx_wkckv"] = inp["L1_xattn_w_kc_kv"].transpose(1, 0, 2)
    a["cx_woT"] = inp["L1_xattn_Wo"].reshape(D, CH, CK).transpose(2, 1, 0)

    def angles(n, dim):
        inv = f(1.0) / f(10000.0) ** (np.arange(0, dim, 2, dtype=f) / f(dim))
        g = np.arange(n, dtype=f)[:, None] * inv[None, :].astype(f)
        return np.repeat(np.cos(g), 2, axis=1).astype(f), np.repeat(np.sin(g), 2, axis=1).astype(f)

    cos, sin = angles(S, CQ)
    sin = np.roll(sin, HALF, axis=1) * np.where(np.arange(CQ) < HALF, 1.0, -1.0).astype(f)
    tab = np.stack([cos.T, sin.T], axis=0)
    lo, hi = tab[:, 0:P], tab[:, P:CQ]
    a["cx_tab"] = np.stack([lo, np.concatenate([hi, hi], axis=1), lo], axis=2).transpose(1, 0, 2, 3)
    cos, sin = angles(SK, DCX)
    sin = sin * np.where(np.arange(DCX) < DCX // 2, -1.0, 1.0).astype(f)
    at = np.minimum(np.arange(SKP), SK - 1)
    a["cx_kcos"], a["cx_ksin"] = cos[at].T, sin[at].T
    ctxT = inp["ctx_512"][:, at, :].transpose(0, 2, 1)
    a["cx_ctxT"] = ctxT
    a["cx_ctxrT"] = np.roll(ctxT, DCX // 2, axis=1)


def quantise_rows(dve, step, rows, q_out, amax, inv, back, tmp, signal):
    step.each(lambda g: dve.tensor_reduce(amax[g], rows[g], AX.X, ALU.max, apply_absolute_value=True))
    step.each(lambda g: dve.tensor_scalar(amax[g], amax[g], 1e-5, None, ALU.max))
    for g in range(SLOTS):
        dve.tensor_scalar(back[g], amax[g], 1.0 / 127.0, None, ALU.mult)
    step.each(lambda g: dve.reciprocal(inv[g], amax[g]))
    step.each(lambda g: dve.tensor_scalar(inv[g], inv[g], 127.0, None, ALU.mult))
    step.each(lambda g: dve.tensor_scalar(tmp[g], rows[g], inv[g], ROUND, ALU.mult, ALU.add))
    step.each(lambda g: dve.tensor_scalar(tmp[g], tmp[g], ROUND, 127.0, ALU.subtract, ALU.min))
    for g in range(SLOTS):
        dve.tensor_scalar(q_out[g], tmp[g], -128.0, None, ALU.max).then_inc(signal, 1)


def quantised_mlp(nc, sb, pb, sem, a, x_all, const, sem_later, later):
    ident = const["ident"]
    name = "f0"
    G = range(SLOTS)
    FC = FF // P
    w1T = sb("f0_w1T", [P, DC, FF], BF16)
    w2T = sb("f0_w2T", [P, FC, D], BF16)
    s1row = sb("f0_s1row", [P, FF])
    s2row = sb("f0_s2row", [P, D])
    identb = sb("f0_identb", [P, P], BF16)

    with ExitStack() as prep:
        def psb(nm, shape, dt=F32):
            return prep.enter_context(nc.sbuf_tensor(nm, shape, dt))

        def ppb(nm, shape, dt=F32):
            return prep.enter_context(nc.psum_tensor(nm, shape, dt))
        w1 = psb("f0_w1", [P, FC, D])
        w2 = psb("f0_w2", [P, DC, FF])
        asum = psb("f0_asum", [P, FC + DC])
        rec = psb("f0_rec", [P, FC + DC])
        q1 = psb("f0_q1", [P, FC, D], BF16)
        q2 = psb("f0_q2", [P, DC, FF], BF16)
        diag = psb("f0_diag", [P, FC + DC, P])
        ones = psb("f0_ones", [P, P])
        w1ps = ppb("f0_w1ps", [P, DC, FF], BF16)
        w2ps = ppb("f0_w2ps", [P, FC, D], BF16)
        s1ps = ppb("f0_s1ps", [P, FF])
        s2ps = ppb("f0_s2ps", [P, D])
        load(nc, sem("f0_loaded"), [(w1[:, :, :], a["f0_w1"]), (w2[:, :, :], a["f0_w2"])], sem_later, later)
        s_step = sem("f0_prep_step")
        s_q1 = sem("f0_w_quantised")
        s_ps = sem("f0_w_turned")
        with nc.Block() as block:

            @block.vector
            def _(dve):
                step = Steps(dve, s_step)
                dve.memset(ones[:, :], 1.0)
                dve.tensor_copy(identb[:, :], ident[:, :])
                for w, q, lo, n, width in ((w1, q1, 0, FC, D), (w2, q2, FC, DC, FF)):
                    sc, rc = asum[:, lo:lo + n], rec[:, lo:lo + n]
                    step.done(dve.tensor_reduce(sc, w[:, :, :], AX.X, ALU.add, apply_absolute_value=True))
                    step.done(dve.tensor_scalar(sc, sc, 1.0 / width, 1e-5, ALU.mult, ALU.max))
                    step.done(dve.reciprocal(rc, sc))
                    step.done(dve.tensor_tensor(w[:, :, :], w[:, :, :], rc.unsqueeze(2).broadcast_to([P, n, width]),
                                                ALU.mult))
                    step.done(dve.tensor_scalar(w[:, :, :], w[:, :, :], ROUND, ROUND, ALU.add, ALU.subtract))
                    step.done(dve.tensor_scalar(q[:, :, :], w[:, :, :], 1.0, -1.0, ALU.min, ALU.max))
                    for i in range(n):
                        last = dve.tensor_scalar(diag[:, lo + i, :], ident[:, :], asum[:, lo + i:lo + i + 1], None,
                                                 ALU.mult)
                last.then_inc(s_q1, 1)
                dve.wait_ge(s_ps, 1)
                dve.tensor_copy(w1T[:, :, :], w1ps[:, :, :])
                dve.tensor_copy(w2T[:, :, :], w2ps[:, :, :])
                dve.tensor_copy(s1row[:, :], s1ps[:, :])
                dve.tensor_copy(s2row[:, :], s2ps[:, :]).then_inc(s_step, 1)

            @block.tensor
            def _(pe):
                pe.wait_ge(s_q1, 1)
                for i in range(FC):
                    for c in range(DC):
                        pe.transpose(w1ps[:, c, i * P:(i + 1) * P], q1[:, i, c * P:(c + 1) * P], identb[:, :])
                        pe.transpose(w2ps[:, i, c * P:(c + 1) * P], q2[:, c, i * P:(i + 1) * P], identb[:, :])
                for i in range(FC):
                    pe.matmul(s1ps[:, i * P:(i + 1) * P], ones[:, :], diag[:, i, :], start=True, stop=True)
                for i in range(DC):
                    last = pe.matmul(s2ps[:, i * P:(i + 1) * P], ones[:, :], diag[:, FC + i, :], start=True, stop=True)
                last.then_inc(s_ps, 1)

    stats = [sb(f"{name}_stats{g}", [P, 6]) for g in G]
    mv = [sb(f"{name}_mv{g}", [P, 3]) for g in G]
    rstd = [sb(f"{name}_rstd{g}", [P, 1]) for g in G]
    xn = [sb(f"{name}_xn{g}", [P, D]) for g in G]
    amax = [sb(f"{name}_amax{g}", [P, 2]) for g in G]
    inv = [sb(f"{name}_inv{g}", [P, 2]) for g in G]
    back = [sb(f"{name}_back{g}", [P, 2]) for g in G]
    y1 = [sb(f"{name}_y1{g}", [P, D], BF16) for g in G]
    y1T = [sb(f"{name}_y1T{g}", [P, DC, P], BF16) for g in G]
    hid = [sb(f"{name}_hid{g}", [P, FF]) for g in G]
    tmp = [sb(f"{name}_tmp{g}", [P, FF]) for g in G]
    y2 = [sb(f"{name}_y2{g}", [P, FF], BF16) for g in G]
    y2T = [sb(f"{name}_y2T{g}", [P, FC, P], BF16) for g in G]
    front = [pb(f"{name}_front{g}", [P, 512]) for g in G]
    up = [pb(f"{name}_up{g}", [P, FF]) for g in G]
    turned = [pb(f"{name}_turned{g}", [P, FC, P], BF16) for g in G]

    s_var = sem("f0_variance")
    s_rstd = sem("f0_rstd")
    s_y1 = sem("f0_y1_quantised")
    s_y1T = sem("f0_y1_turned")
    s_y1Tc = sem("f0_y1T_kept")
    s_up = sem("f0_up")
    s_hid = sem("f0_hidden")
    s_gelu = sem("f0_gelu")
    s_y2 = sem("f0_y2_quantised")
    s_y2T = sem("f0_y2_turned")
    s_y2Tc = sem("f0_y2T_kept")
    s_down = sem("f0_down")
    s_x = sem("f0_x_updated")
    s_dve = sem("f0_dve_step")
    steps_ahead, dve_steps = 9, 16

    with nc.Block() as block:

        @block.gpsimd
        def _(pool):
            with pool.Fori(0, ROUNDS) as r:
                for g in G:
                    pool.wait_ge(s_var, r * SLOTS + g + 1)
                    pool.tensor_tensor(rstd[g][:, :], mv[g][:, 1:2], const["minus_half"][:, 0:1], ALU.pow)\
                        .then_inc(s_rstd, 1)

        @block.tensor
        def _(pe):
            def turn_y1(r, g):
                pe.wait_ge(s_y1, r * SLOTS + g + 1)
                for c in range(DC):
                    last = pe.transpose(turned[g][:, c, :], y1[g][:, c * P:(c + 1) * P], identb[:, :])
                last.then_inc(s_y1T, 1)

            def up_product(r, g):
                pe.wait_ge(s_y1Tc, r * SLOTS + g + 1)
                if not (isinstance(r, int) and r == 0):
                    pe.wait_ge(s_hid, (r - 1) * SLOTS + g + 1)
                for n in range(2):
                    for c in range(DC):
                        last = pe.matmul(up[g][:, n * 512:(n + 1) * 512], y1T[g][:, c, :],
                                         w1T[:, c, n * 512:(n + 1) * 512], start=(c == 0), stop=(c == DC - 1))
                last.then_inc(s_up, 1)

            def turn_y2(r, g):
                pe.wait_ge(s_y2, r * SLOTS + g + 1)
                for i in range(FC):
                    last = pe.transpose(turned[g][:, i, :], y2[g][:, i * P:(i + 1) * P], identb[:, :])
                last.then_inc(s_y2T, 1)

            def down_product(r, g):
                pe.wait_ge(s_y2Tc, r * SLOTS + g + 1)
                if not (isinstance(r, int) and r == 0):
                    pe.wait_ge(s_x, r * SLOTS)
                for i in range(FC):
                    last = pe.matmul(front[g][:, 0:D], y2T[g][:, i, :], w2T[:, i, :], start=(i == 0), stop=(i == FC - 1))
                last.then_inc(s_down, 1)

            rounds(pe, (turn_y1, up_product), ((turn_y1, 1), (up_product, 1), (turn_y2, 0), (down_product, 0)))

        @block.scalar
        def _(act):
            def keep_y1T(r, g):
                act.wait_ge(s_y1T, r * SLOTS + g + 1)
                act.copy(y1T[g][:, :, :], turned[g][:, 0:DC, :]).then_inc(s_y1Tc, 1)

            def gelu(r, g):
                act.wait_ge(s_hid, r * SLOTS + g + 1)
                act.activation(hid[g][:, :], hid[g][:, :], ACT.Gelu_apprx_tanh).then_inc(s_gelu, 1)

            def keep_y2T(r, g):
                act.wait_ge(s_y2T, r * SLOTS + g + 1)
                act.copy(y2T[g][:, :, :], turned[g][:, :, :]).then_inc(s_y2Tc, 1)

            rounds(act, (keep_y1T, gelu), ((keep_y1T, 1), (keep_y2T, 0), (gelu, 1)))

        @block.vector
        def _(dve):
            step = Steps(dve, s_dve)

            def normalise(r, slot):
                if slot:
                    return
                x = [x_all[:, bass.ds(r * SLOTS + g, 1), :] for g in G]
                step.each(lambda g: dve.bn_stats(stats[g][:, :], x[g]))
                dve.memset(mv[0][:, 2:3], 0.0)
                step.each(lambda g: dve.bn_aggr(mv[g][:, 0:2], stats[g][:, :]))
                for g in G:
                    dve.tensor_scalar(mv[g][:, 1:2], mv[g][:, 1:2], EPS, None, ALU.add).then_inc(s_var, 1)
                dve.wait_ge(s_rstd, r * SLOTS + SLOTS)
                step.each(lambda g: dve.tensor_scalar(xn[g][:, :], x[g], mv[g][:, 0:1], rstd[g][:, 0:1],
                                                      ALU.subtract, ALU.mult))
                quantise_rows(dve, step, [xn[g][:, :] for g in G], [y1[g][:, :] for g in G],
                              [amax[g][:, 0:1] for g in G], [inv[g][:, 0:1] for g in G],
                              [back[g][:, 0:1] for g in G], [tmp[g][:, 0:D] for g in G], s_y1)

            def hidden(r, g):
                dve.wait_ge(s_up, r * SLOTS + g + 1)
                dve.scalar_tensor_tensor(out=hid[g][:, :], in0=up[g][:, :], scalar=back[g][:, 0:1], in1=s1row[:, :],
                                         op0=ALU.mult, op1=ALU.mult).then_inc(s_hid, 1)

            def quantise_hidden(r, slot):
                if slot:
                    return
                dve.wait_ge(s_gelu, r * SLOTS + SLOTS)
                quantise_rows(dve, step, [hid[g][:, :] for g in G], [y2[g][:, :] for g in G],
                              [amax[g][:, 1:2] for g in G], [inv[g][:, 1:2] for g in G],
                              [back[g][:, 1:2] for g in G], [tmp[g][:, :] for g in G], s_y2)

            def update_x(r, g):
                if g:
                    return
                dve.wait_ge(s_down, r * SLOTS + SLOTS)
                step.each(lambda g: dve.scalar_tensor_tensor(
                    out=tmp[g][:, 0:D], in0=front[g][:, 0:D], scalar=back[g][:, 1:2], in1=s2row[:, :],
                    op0=ALU.mult, op1=ALU.mult))
                for g in G:
                    x = x_all[:, bass.ds(r * SLOTS + g, 1), :]
                    dve.tensor_tensor(x, tmp[g][:, 0:D].unsqueeze(1), x, ALU.add).then_inc(s_x, 1)

            step.start(0)
            rounds(dve, (normalise, hidden), ((normalise, 1), (quantise_hidden, 0), (hidden, 1), (update_x, 0)),
                   lambda r: step.start(r * dve_steps + steps_ahead))


E, TOPK, FE = 16, 4, 176
NE = 20
NF = NE * FE
NFC = -(-NF // P)


def experts_weights(sb, a):
    wgu = sb("moe_wgu", [P, NE, DC, 2 * FE])
    wd = sb("moe_wd", [P, NFC, D])
    wr = sb("moe_wr", [P, DC, E + 1])
    before = sb("moe_before", [P, E, E])
    pairs = [(wr[:, :, :], a["moe_wr"]), (before[:, :, :], a["moe_before"])]
    pairs += [(wgu[:, 4 * i:4 * i + 4], a["moe_wgu"][:, 4 * i:4 * i + 4]) for i in range(NE // 4)]
    pairs += [(wd[:, 7 * i:7 * i + 7, :], a["moe_wd"][:, 7 * i:7 * i + 7, :]) for i in range(NFC // 7)]
    return (wgu, wd, wr, before), pairs


def experts_mlp(nc, sb, pb, sem, x_all, const, wgu, wd, wr, before):
    ident = const["ident"]
    G = range(SLOTS)
    stats = [sb(f"moe_stats{g}", [P, 6]) for g in G]
    mv = [sb(f"moe_mv{g}", [P, 3]) for g in G]
    rstd = [sb(f"moe_rstd{g}", [P, 1]) for g in G]
    xn = [sb(f"moe_xn{g}", [P, D]) for g in G]
    xnT = [sb(f"moe_xnT{g}", [P, DC, P]) for g in G]
    logit = [sb(f"moe_logit{g}", [P, E + 1]) for g in G]
    nmax = [sb(f"moe_nmax{g}", [P, 1]) for g in G]
    rw = [sb(f"moe_rw{g}", [P, E + 1]) for g in G]
    rsum = [sb(f"moe_rsum{g}", [P, 1]) for g in G]
    ahead = [sb(f"moe_ahead{g}", [P, E, E]) for g in G]
    equal = [sb(f"moe_equal{g}", [P, E, E]) for g in G]
    rank = [sb(f"moe_rank{g}", [P, E]) for g in G]
    coef = [sb(f"moe_coef{g}", [P, E + 1]) for g in G]
    RING = 3
    silu = [sb(f"moe_silu{i}", [P, FE]) for i in range(RING)]
    hid = sb("moe_hid", [P, NF])
    hidT = [sb(f"moe_hidT{i}", [P, 4, P]) for i in range(2)]
    gu = [pb(f"moe_gu{i}", [P, 512]) for i in range(RING)]
    turned = [pb(f"moe_turned{i}", [P, 4, P]) for i in range(2)]
    front = pb("moe_front", [P, 512])
    acc = pb("moe_acc", [P, 512])

    NQ = NFC // 4
    LAST = [min(-(-(512 * (q + 1)) // FE), NE) - 1 for q in range(NQ)]
    TURN = {min(LAST[q] + 2, NE): q for q in range(NQ)}
    s_var = sem("moe_variance")
    s_rstd = sem("moe_rstd")
    s_xn = sem("moe_normalised")
    s_xT = sem("moe_x_turned")
    s_xTc = sem("moe_xT_kept")
    s_rl = sem("moe_router_logits")
    s_lg = sem("moe_logits_kept")
    s_rx = sem("moe_router_exp")
    s_cf = sem("moe_coefficients")
    s_gu = sem("moe_gate_up")
    s_silu = sem("moe_silu_done")
    s_hid = sem("moe_hidden")
    s_turn = sem("moe_hidden_turned")
    s_turnc = sem("moe_hiddenT_kept")
    s_acc = sem("moe_down")
    s_x = sem("moe_x_updated")
    s_dve = sem("moe_dve_step")
    FRONT_STEPS = 9

    def rounds(engine, tile):
        with engine.Fori(0, ROUNDS - 1) as r:
            for g in G:
                tile(r * SLOTS + g, g, True)
        for g in G:
            tile((ROUNDS - 1) * SLOTS + g, g, g + 1 < SLOTS)

    with nc.Block() as block:

        @block.gpsimd
        def _(pool):
            def root(t, g):
                pool.wait_ge(s_var, t + 1)
                pool.tensor_tensor(rstd[g][:, :], mv[g][:, 1:2], const["minus_half"][:, 0:1], ALU.pow)\
                    .then_inc(s_rstd, 1)

            def tile(t, g, follows):
                if follows:
                    root(t + 1, 1 - g)

            root(0, 0)
            rounds(pool, tile)

        @block.tensor
        def _(pe):
            pe.sem_inc(s_turn, LEAD)

            def turn_x(t, g):
                pe.wait_ge(s_xn, t + 1)
                for c in range(DC):
                    last = pe.transpose(front[:, c * P:(c + 1) * P], xn[g][:, c * P:(c + 1) * P], ident[:, :])
                last.then_inc(s_xT, 1)

            def router(t, g):
                pe.wait_ge(s_xTc, t + 1)
                for c in range(DC):
                    last = pe.matmul(front[:, 0:E + 1], xnT[g][:, c, :], wr[:, c, :],
                                     start=(c == 0), stop=(c == DC - 1))
                last.then_inc(s_rl, 1)

            def gate_up(t, g, e):
                if e >= RING:
                    pe.wait_ge(s_hid, LEAD + t * NE + e - RING + 1)
                else:
                    pe.wait_ge(s_hid, LEAD + t * NE)
                i = e % RING
                for c in range(DC):
                    last = pe.matmul(gu[i][:, 0:2 * FE], xnT[g][:, c, :], wgu[:, e, c, :],
                                     start=(c == 0), stop=(c == DC - 1))
                last.then_inc(s_gu, 1)

            def turn(t, q):
                pe.wait_ge(s_hid, LEAD + t * NE + LAST[q] + 1)
                if q >= 2:
                    pe.wait_ge(s_turnc, LEAD + t * NQ + q - 1)
                else:
                    pe.wait_ge(s_turnc, LEAD + t * NQ)
                for k in range(4 * q, 4 * q + 4):
                    n = min(P, NF - k * P)
                    last = pe.transpose(turned[q % 2][0:n, k % 4, :], hid[:, k * P:k * P + n], ident[:, :])
                last.then_inc(s_turn, 1)

            def down(t, q):
                pe.wait_ge(s_turnc, LEAD + t * NQ + q + 1)
                if q == 0:
                    pe.wait_ge(s_x, LEAD + t)
                for k in range(4 * q, 4 * q + 4):
                    n = min(P, NF - k * P)
                    last = pe.matmul(acc[:, 0:D], hidT[q % 2][0:n, k % 4, :], wd[0:n, k, :],
                                     start=(k == 0), stop=(k == NFC - 1))
                if q == NQ - 1:
                    last.then_inc(s_acc, 1)

            def tile(t, g, follows):
                for e in range(NE):
                    gate_up(t, g, e)
                    if e in TURN:
                        turn(t, TURN[e])
                        if TURN[e] >= 1:
                            down(t, TURN[e] - 1)
                if follows:
                    turn_x(t + 1, 1 - g)
                turn(t, NQ - 1)
                down(t, NQ - 2)
                if follows:
                    router(t + 1, 1 - g)
                down(t, NQ - 1)

            turn_x(0, 0)
            router(0, 0)
            rounds(pe, tile)

        @block.scalar
        def _(act):
            act.sem_inc(s_turnc, LEAD)

            def keep_xT(t, g):
                act.wait_ge(s_xT, t + 1)
                act.copy(xnT[g][:, :, :], front[:, 0:D]).then_inc(s_xTc, 1)

            def router_exp(t, g):
                act.wait_ge(s_lg, t + 1)
                act.activation(rw[g][:, 0:E], logit[g][:, 0:E], ACT.Exp, bias=nmax[g][:, 0:1],
                               accum_out=rsum[g][:, 0:1])
                act.activation(rw[g][:, E:E + 1], logit[g][:, E:E + 1], ACT.Exp, scale=-1.0).then_inc(s_rx, 1)

            def silus(t, e):
                act.wait_ge(s_gu, t * NE + e + 1)
                act.activation(silu[e % RING][:, :], gu[e % RING][:, 0:FE], ACT.Silu).then_inc(s_silu, 1)

            def tile(t, g, follows):
                for e in range(NE):
                    silus(t, e)
                    if e in TURN:
                        keep(t, TURN[e])
                if follows:
                    keep_xT(t + 1, 1 - g)
                keep(t, NQ - 1)
                if follows:
                    router_exp(t + 1, 1 - g)

            def keep(t, q):
                act.wait_ge(s_turn, LEAD + t * NQ + q + 1)
                whole = [k for k in range(4) if (4 * q + k + 1) * P <= NF]
                last = act.copy(hidT[q % 2][:, 0:len(whole), :], turned[q % 2][:, 0:len(whole), :])
                if len(whole) < 4:
                    m = NF % P
                    last = act.copy(hidT[q % 2][0:m, 3, :], turned[q % 2][0:m, 3, :])
                last.then_inc(s_turnc, 1)

            keep_xT(0, 0)
            router_exp(0, 0)
            rounds(act, tile)

        @block.vector
        def _(dve):
            step = Steps(dve, s_dve)
            dve.sem_inc(s_hid, LEAD)
            dve.sem_inc(s_x, LEAD)

            def normalise(t, g):
                x = x_all[:, bass.ds(t, 1), :]
                step.done(dve.bn_stats(stats[g][:, :], x))
                dve.memset(mv[g][:, 2:3], 0.0)
                step.done(dve.bn_aggr(mv[g][:, 0:2], stats[g][:, :]))
                dve.tensor_scalar(mv[g][:, 1:2], mv[g][:, 1:2], EPS, None, ALU.add).then_inc(s_var, 1)
                dve.wait_ge(s_rstd, t + 1)
                dve.tensor_scalar(xn[g][:, :], x, mv[g][:, 0:1], rstd[g][:, 0:1], ALU.subtract, ALU.mult)\
                    .then_inc(s_xn, 1)

            def logits(t, g):
                dve.wait_ge(s_rl, t + 1)
                step.done(dve.tensor_copy(logit[g][:, :], front[:, 0:E + 1]))
                dve.tensor_reduce(nmax[g][:, :], logit[g][:, 0:E], AX.X, ALU.max, negate=True).then_inc(s_lg, 1)

            def coefficients(t, g):
                dve.wait_ge(s_rx, t + 1)
                dve.tensor_scalar(rw[g][:, E:E + 1], rw[g][:, E:E + 1], 1.0, None, ALU.add)
                step.done(dve.reciprocal(rsum[g][:, :], rsum[g][:, :]))
                dve.reciprocal(coef[g][:, E:E + 1], rw[g][:, E:E + 1])
                step.done(dve.tensor_scalar(rw[g][:, 0:E], rw[g][:, 0:E], rsum[g][:, 0:1], None, ALU.mult))
                other = rw[g][:, 0:E].unsqueeze(1).broadcast_to([P, E, E])
                own = rw[g][:, 0:E].unsqueeze(2).broadcast_to([P, E, E])
                step.done(dve.tensor_tensor(equal[g][:, :, :], other, own, ALU.is_equal))
                dve.tensor_tensor(ahead[g][:, :, :], other, own, ALU.is_gt)
                step.done(dve.tensor_tensor(equal[g][:, :, :], equal[g][:, :, :], before[:, :, :], ALU.mult))
                step.done(dve.tensor_tensor(ahead[g][:, :, :], ahead[g][:, :, :], equal[g][:, :, :], ALU.add))
                step.done(dve.tensor_reduce(rank[g][:, :], ahead[g][:, :, :], AX.X, ALU.add))
                dve.scalar_tensor_tensor(out=coef[g][:, 0:E], in0=rank[g][:, :], scalar=float(TOPK), in1=rw[g][:, 0:E],
                                         op0=ALU.is_lt, op1=ALU.mult).then_inc(s_cf, 1)

            def hidden(t, g, e):
                dve.wait_ge(s_silu, t * NE + e + 1)
                k = min(e, E)
                if e == 0:
                    dve.wait_ge(s_cf, t + 1)
                    dve.wait_ge(s_turn, LEAD + t * NQ)
                dve.scalar_tensor_tensor(out=hid[:, e * FE:(e + 1) * FE], in0=silu[e % RING][:, :],
                                         scalar=coef[g][:, k:k + 1], in1=gu[e % RING][:, FE:2 * FE],
                                         op0=ALU.mult, op1=ALU.mult).then_inc(s_hid, 1)

            def update_x(t):
                dve.wait_ge(s_acc, t + 1)
                x = x_all[:, bass.ds(t, 1), :]
                dve.tensor_tensor(x, acc[:, 0:D].unsqueeze(1), x, ALU.add).then_inc(s_x, 1)

            def tile(t, g, follows):
                for e in range(NE):
                    hidden(t, g, e)
                    if e == NE // 2 and follows:
                        step.start(t * FRONT_STEPS + FRONT_STEPS)
                        normalise(t + 1, 1 - g)
                if follows:
                    logits(t + 1, 1 - g)
                    coefficients(t + 1, 1 - g)
                    assert step.n == FRONT_STEPS, step.n
                update_x(t)

            normalise(0, 0)
            logits(0, 0)
            coefficients(0, 0)
            rounds(dve, tile)


def more_layout(inp, a, rows, spread):
    context_layout(inp, a, rows, spread)
    f = np.float32
    a["f0_w1"] = inp["L0_ffn_w1"].reshape(FF // P, P, D).transpose(1, 0, 2)
    a["f0_w2"] = inp["L0_ffn_w2"].reshape(D // P, P, FF).transpose(1, 0, 2)
    a["moe_wr"] = rows(np.concatenate([inp["L1_ffn_gate_w"], inp["L1_ffn_sgate_w"]], axis=0))
    j, e = np.arange(E)[None, :], np.arange(E)[:, None]
    a["moe_before"] = spread((j < e).astype(f))
    sgu = inp["L1_ffn_shared_gate_up_w"].reshape(2, NE - E, FE, D).transpose(1, 0, 2, 3).reshape(NE - E, 2 * FE, D)
    wgu = np.concatenate([inp["L1_ffn_w13"], sgu], axis=0)
    a["moe_wgu"] = wgu.reshape(NE, 2 * FE, DC, P).transpose(3, 0, 2, 1)
    wd = np.concatenate([inp["L1_ffn_w2"].transpose(0, 2, 1).reshape(E * FE, D), inp["L1_ffn_shared_down_w"].T,
                         np.zeros((NFC * P - NF, D), f)], axis=0)
    a["moe_wd"] = wd.reshape(NFC, P, D).transpose(1, 0, 2)


def load(nc, sem_loaded, pairs, sem_later=None, later=()):
    with nc.Block() as block:

        @block.sync
        def _(sp):
            for dst, src in pairs[0::2]:
                sp.dma_start(dst, src).then_inc(sem_loaded, 16)
            for dst, src in later:
                sp.dma_start(dst, src).then_inc(sem_later, 16)
            sp.wait_ge(sem_loaded, 16 * len(pairs))

        @block.scalar
        def _(act):
            for dst, src in pairs[1::2]:
                act.dma_start(dst, src).then_inc(sem_loaded, 16)


def await_load(nc, sem_loaded, pairs):
    with nc.Block() as block:

        @block.sync
        def _(sp):
            sp.wait_ge(sem_loaded, 16 * len(pairs))


def attention_weights(sb, a, phase, kind):
    shapes = {"o": [P, DC, D]}
    if kind == "context":
        shapes |= {"q": [P, DC, D], "k": [DCX, D], "v": [DCX, D], "ctx": [DCX, B * S]}
    else:
        shapes |= {"qk": [P, DC, 2 * D], "v": [P, DC, D]}
    if kind == "bias":
        shapes |= {"bqk": [P, 2 * D], "bv": [P, D], "bo": [P, D]}
    if kind == "rope":
        shapes |= {"cos": [P, 2 * D], "sin": [P, 2 * D]}
    w = {key: sb(f"{phase}_w{key}", shape) for key, shape in shapes.items()}
    return w, [(w[key][tuple(slice(None) for _ in shape)], a[f"{phase}_{key}"]) for key, shape in shapes.items()]


def perceiver(nc, a, out):
    with ExitStack() as whole:
        semaphores = {}

        def sem(name):
            if name not in semaphores:
                semaphores[name] = whole.enter_context(nc.semaphore(name))
            return semaphores[name]

        def holder(stack):
            def sb(name, shape, dt=F32):
                return stack.enter_context(nc.sbuf_tensor(name, shape, dt))

            def pb(name, shape, dt=F32):
                return stack.enter_context(nc.psum_tensor(name, shape, dt))
            return sb, pb

        sb, _ = holder(whole)
        x_all = sb("x_all", [P, NT, D])
        const = {
            "ident": sb("ident", [P, P]),
            "mask": sb("mask", [P, S]),
            "head_rows": sb("head_rows", [P, H // 2]),
            "minus_half": sb("minus_half", [P, 1]),
        }
        pairs = [(x_all[:, :, :], a["x"].rearrange("(t p) d -> p t d", p=P))]
        pairs += [(const[k][:, :], a[k]) for k in const]
        load(nc, sem("s_const_loaded"), pairs)

        nth, steps = 0, 0
        for phase, later in GROUPS:
            with ExitStack() as later_stack, ExitStack() as prep:
                later_sb, later_pb = holder(later_stack)
                later_pairs, sem_later = [], None
                if later == "cx":
                    kept, raw, later_pairs = context_weights(later_sb, holder(prep)[0], a)
                elif later == "moe":
                    kept, later_pairs = experts_weights(later_sb, a)
                if later:
                    sem_later = sem(f"s_{later}_loaded")
                with ExitStack() as stack:
                    sb, pb = holder(stack)
                    if phase == "f0":
                        quantised_mlp(nc, sb, pb, sem, a, x_all, const, sem_later, later_pairs)
                    else:
                        kind = {"a0": "context", "a1": "bias", "a2": "rope"}[phase]
                        w, pairs = attention_weights(sb, a, phase, kind)
                        load(nc, sem(f"s_{phase}_loaded"), pairs, sem_later, later_pairs)
                        steps = small_attention(nc, sb, pb, sem, kind, phase, w, x_all, const, nth, steps)
                        nth += 1
                if later:
                    await_load(nc, sem_later, later_pairs)
                if later == "cx":
                    absorb_weights(nc, sem, raw, *kept)
                prep.close()
                if later == "cx":
                    context_attention(nc, later_sb, later_pb, sem, a, x_all, const, *kept)
                elif later == "moe":
                    experts_mlp(nc, later_sb, later_pb, sem, x_all, const, *kept)

        s_out = sem("s_out")
        with nc.Block() as block:

            @block.sync
            def _(sp):
                sp.dma_start(out.rearrange("(t p) d -> p t d", p=P), x_all[:, :, :]).then_inc(s_out, 16)
                sp.wait_ge(s_out, 16)


GROUPS = (("a0", None), ("a1", None), ("f0", "cx"), ("a2", "moe"))


def _layout(inp):
    f = np.float32

    def rows(m):
        n, k = m.shape
        return m.T.reshape(k // P, P, n).transpose(1, 0, 2)

    def spread(v):
        return np.broadcast_to(v, (P,) + v.shape)

    a = {"x": inp["x"].reshape(B * S, D)}
    a["ident"] = np.eye(P, dtype=f)
    q, k = np.arange(P)[:, None] % S, np.arange(S)[None, :]
    a["mask"] = np.where(k <= q, 0.0, np.finfo(f).min).astype(f)
    a["head_rows"] = (np.arange(P)[:, None] // DH == np.arange(H // 2)[None, :]).astype(f)
    a["minus_half"] = np.full((P, 1), -0.5, f)

    a["a0_q"] = rows(inp["L0_xattn_Wq"])
    a["a0_k"] = inp["L0_xattn_Wkv_expand"][0:D].T
    a["a0_v"] = inp["L0_xattn_Wkv_expand"][D:].T
    a["a0_ctx"] = inp["ctx_512"][:, 0:S, :].transpose(2, 0, 1).reshape(DCX, B * S)
    a["a0_o"] = rows(inp["L0_xattn_Wout"])
    for ph, src in (("a1", "L0_attn"), ("a2", "L1_attn")):
        a[f"{ph}_qk"] = np.concatenate([rows(inp[f"{src}_Wq"]), rows(inp[f"{src}_Wk"])], axis=2)
        a[f"{ph}_v"] = rows(inp[f"{src}_Wv"])
        a[f"{ph}_o"] = rows(inp[f"{src}_Wo"])
    a["a1_bqk"] = spread(np.concatenate([inp["L0_attn_bq"], inp["L0_attn_bk"]]))
    a["a1_bv"] = spread(inp["L0_attn_bv"])
    a["a1_bo"] = spread(inp["L0_attn_bo"])
    theta = f(10000.0) ** (f(-2.0) * np.arange(DH // 2, dtype=f) / f(DH))
    angle = (np.arange(P) % S).astype(f)[:, None] * theta[None, :].astype(f)
    cos, sin = np.cos(angle).astype(f), np.sin(angle).astype(f)
    a["a2_cos"] = np.tile(np.repeat(cos, 2, axis=1), (1, 2 * H))
    a["a2_sin"] = np.tile(np.stack([-sin, sin], axis=2).reshape(P, DH), (1, 2 * H))
    more_layout(inp, a, rows, spread)
    return {k: np.ascontiguousarray(v) for k, v in a.items()}


def kernel(**inputs):
    import concourse.bacc as bacc
    from concourse.bass_utils import run_bass_kernel_spmd

    nc = bacc.Bacc("TRN2", target_bir_lowering=False, num_devices=1)
    arrays = _layout({k: np.asarray(v) for k, v in inputs.items()})
    aps = {k: nc.dram_tensor(f"in_{k}", v.shape, mybir.dt.from_np(v.dtype), kind="ExternalInput").ap()
           for k, v in arrays.items()}
    out = nc.dram_tensor("out_x", (B * S, D), F32, kind="ExternalOutput").ap()
    perceiver(nc, aps, out)
    r = run_bass_kernel_spmd(nc, [{f"in_{k}": v for k, v in arrays.items()}], core_ids=[0])
    return r.results[0]["out_x"].reshape(B, S, D)
```
